# Optimizing a Trainium2 kernel written in Bass

```python
import numpy as np
import jax
import jax.numpy as jnp

def _softmax(x, axis=-1):
    return jax.nn.softmax(x, axis=axis)

def _gelu(x):
    return jax.nn.gelu(x, approximate=True)

def _silu(x):
    return jax.nn.silu(x)

def _sigmoid(x):
    return jax.nn.sigmoid(x)

def _layernorm(x, axis=-1, eps=1e-05):
    m = jnp.mean(x, axis=axis, keepdims=True)
    v = jnp.var(x, axis=axis, keepdims=True)
    return (x - m) / jnp.sqrt(v + eps)

def _scatter_add(tgt, idx, src, axis=0):
    return tgt.at[idx].add(src)

def _segment_sum(src, seg, n):
    return jax.ops.segment_sum(src, seg, n)
kernel_name = 'mk_gnn_resnorm_d2_gnn_r32_b79588'

def setup_inputs(seed: int=0):
    np.random.seed(seed)
    _w = jnp.asarray

    def _rec_inputs():
        import jax
        import jax.numpy as jnp
        _gk = jax.random.key(seed)
        x = -0.0005963 + 1.001 * jax.random.normal(jax.random.fold_in(_gk, 1), (96, 1024), jnp.float32)
        src = jax.random.randint(jax.random.fold_in(_gk, 2), (1536,), 0, 96, jnp.int32)
        dst = jnp.minimum((96 * jax.random.uniform(jax.random.fold_in(_gk, 3), (1536,)) ** 2.0).astype(jnp.int32), 3071)
        _o = jnp.argsort(dst, stable=True)
        src = src[_o]
        dst = dst[_o]
        edge_type_5 = jax.random.randint(jax.random.fold_in(_gk, 12), (1536,), 0, 5, jnp.int32)
        edge_type_6 = jax.random.randint(jax.random.fold_in(_gk, 13), (1536,), 0, 6, jnp.int32)
        return (x, src, dst, edge_type_5, edge_type_6)
    x, src, dst, edge_type_5, edge_type_6 = _rec_inputs()

    def _L0_gnn_setup():
        import jax, jax.numpy as jnp
        import numpy as np
        N = 96
        E = 3072
        IN_F = 1024
        OUT_F = 1024
        H = 16
        D = OUT_F // H
        NUM_ETYPES = 4

        def _build_mask(edge_index, edge_type, edge_type_weights, dtype):
            src, dst = (edge_index[0], edge_index[1])
            w = jax.nn.softplus(edge_type_weights)
            mask = jnp.full((N, N), -jnp.inf, dtype=dtype)
            mask = mask.at[src, dst].set(w[edge_type - 1])
            diag = jnp.diagonal(mask)
            idx = jnp.arange(N)
            mask = mask.at[idx, idx].set(jnp.where(jnp.isneginf(diag), w[3], diag))
            return mask
        key = jax.random.key(seed)
        ks = jax.random.split(key, 20)
        p = lambda k, shape: jax.random.normal(k, shape, dtype=jnp.float32) * 0.02
        return {'x': jax.random.normal(ks[0], (N, IN_F), dtype=jnp.float32), 'edge_index': jax.random.randint(ks[1], (2, E), 0, N), 'edge_type': jax.random.randint(ks[2], (E,), 1, NUM_ETYPES + 1), 'edge_type_weights': jnp.ones((NUM_ETYPES,), jnp.float32) + 0.1 * jax.random.normal(ks[3], (NUM_ETYPES,), dtype=jnp.float32), 'wq': p(ks[4], (OUT_F, IN_F)), 'bq': p(ks[5], (OUT_F,)), 'wk': p(ks[6], (OUT_F, IN_F)), 'bk': p(ks[7], (OUT_F,)), 'wv': p(ks[8], (OUT_F, IN_F)), 'bv': p(ks[9], (OUT_F,)), 'wiq': p(ks[10], (OUT_F, OUT_F)), 'biq': p(ks[11], (OUT_F,)), 'wik': p(ks[12], (OUT_F, OUT_F)), 'bik': p(ks[13], (OUT_F,)), 'wiv': p(ks[14], (OUT_F, OUT_F)), 'biv': p(ks[15], (OUT_F,)), 'wo': p(ks[16], (OUT_F, OUT_F)), 'bo': p(ks[17], (OUT_F,))}
    _L0_gnn_all = _L0_gnn_setup()
    _L0_gnn_in = {k: v for k, v in _L0_gnn_all.items() if k in ('edge_type_weights', 'wq', 'bq', 'wk', 'bk', 'wv', 'bv', 'wiq', 'biq', 'wik', 'bik', 'wiv', 'biv', 'wo', 'bo')}
    del _L0_gnn_all

    def _L1_gnn_setup():
        import jax, jax.numpy as jnp
        import numpy as np
        N = 512
        E = 8192
        HID = 1024
        D = 768
        R = 6
        B = 4
        L = 2
        BN_EPS = 1e-05
        LN_EPS = 1e-05

        def _rgcn_conv(x, src, dst, edge_type, basis, comp, root, bias):
            n = x.shape[0]
            W = jnp.einsum('rb,bio->rio', comp, basis)
            h_all = jnp.einsum('ni,rio->rno', x, W)
            counts = jnp.zeros((R, n), x.dtype).at[edge_type, dst].add(1.0)
            norm = 1.0 / counts[edge_type, dst]
            msg = h_all[edge_type, src] * norm[:, None]
            agg = jax.ops.segment_sum(msg, dst, num_segments=n)
            return agg + x @ root + bias

        def _batchnorm(x, gamma, beta):
            mean = jnp.mean(x, axis=0)
            var = jnp.var(x, axis=0)
            return gamma * (x - mean) * jax.lax.rsqrt(var + BN_EPS) + beta

        def _layernorm(x, gamma, beta):
            mean = jnp.mean(x, axis=-1, keepdims=True)
            var = jnp.var(x, axis=-1, keepdims=True)
            return gamma * (x - mean) * jax.lax.rsqrt(var + LN_EPS) + beta
        key = jax.random.key(seed)
        ks = jax.random.split(key, 16)
        s = 0.02
        return {'h_text': jax.random.normal(ks[0], (N, HID), jnp.float32), 'edge_index': jax.random.randint(ks[1], (2, E), 0, N, jnp.int32), 'edge_type': jax.random.randint(ks[2], (E,), 0, R, jnp.int32), 'w_in': jax.random.normal(ks[3], (HID, D), jnp.float32) * s, 'b_in': jnp.zeros((D,), jnp.float32), 'basis': jax.random.normal(ks[4], (L, B, D, D), jnp.float32) * s, 'comp': jax.random.normal(ks[5], (L, R, B), jnp.float32), 'root': jax.random.normal(ks[6], (L, D, D), jnp.float32) * s, 'conv_bias': jnp.zeros((L, D), jnp.float32), 'bn_gamma': jnp.ones((L, D), jnp.float32), 'bn_beta': jnp.zeros((L, D), jnp.float32), 'w_out': jax.random.normal(ks[7], (D, HID), jnp.float32) * s, 'b_out': jnp.zeros((HID,), jnp.float32), 'ln_gamma': jnp.ones((HID,), jnp.float32), 'ln_beta': jnp.zeros((HID,), jnp.float32)}
    _L1_gnn_all = _L1_gnn_setup()
    _L1_gnn_in = {k: v for k, v in _L1_gnn_all.items() if k in ('w_in', 'b_in', 'basis', 'comp', 'root', 'conv_bias', 'bn_gamma', 'bn_beta', 'w_out', 'b_out', 'ln_gamma', 'ln_beta')}
    del _L1_gnn_all
    return {'x': x, 'src': src, 'dst': dst, 'edge_type_5': edge_type_5, 'edge_type_6': edge_type_6, 'L0_gnn_edge_type_weights': _L0_gnn_in['edge_type_weights'], 'L0_gnn_wq': _L0_gnn_in['wq'], 'L0_gnn_bq': _L0_gnn_in['bq'], 'L0_gnn_wk': _L0_gnn_in['wk'], 'L0_gnn_bk': _L0_gnn_in['bk'], 'L0_gnn_wv': _L0_gnn_in['wv'], 'L0_gnn_bv': _L0_gnn_in['bv'], 'L0_gnn_wiq': _L0_gnn_in['wiq'], 'L0_gnn_biq': _L0_gnn_in['biq'], 'L0_gnn_wik': _L0_gnn_in['wik'], 'L0_gnn_bik': _L0_gnn_in['bik'], 'L0_gnn_wiv': _L0_gnn_in['wiv'], 'L0_gnn_biv': _L0_gnn_in['biv'], 'L0_gnn_wo': _L0_gnn_in['wo'], 'L0_gnn_bo': _L0_gnn_in['bo'], 'L1_gnn_w_in': _L1_gnn_in['w_in'], 'L1_gnn_b_in': _L1_gnn_in['b_in'], 'L1_gnn_basis': _L1_gnn_in['basis'], 'L1_gnn_comp': _L1_gnn_in['comp'], 'L1_gnn_root': _L1_gnn_in['root'], 'L1_gnn_conv_bias': _L1_gnn_in['conv_bias'], 'L1_gnn_bn_gamma': _L1_gnn_in['bn_gamma'], 'L1_gnn_bn_beta': _L1_gnn_in['bn_beta'], 'L1_gnn_w_out': _L1_gnn_in['w_out'], 'L1_gnn_b_out': _L1_gnn_in['b_out'], 'L1_gnn_ln_gamma': _L1_gnn_in['ln_gamma'], 'L1_gnn_ln_beta': _L1_gnn_in['ln_beta']}

def reference(x, src, dst, edge_type_5, edge_type_6, L0_gnn_edge_type_weights, L0_gnn_wq, L0_gnn_bq, L0_gnn_wk, L0_gnn_bk, L0_gnn_wv, L0_gnn_bv, L0_gnn_wiq, L0_gnn_biq, L0_gnn_wik, L0_gnn_bik, L0_gnn_wiv, L0_gnn_biv, L0_gnn_wo, L0_gnn_bo, L1_gnn_w_in, L1_gnn_b_in, L1_gnn_basis, L1_gnn_comp, L1_gnn_root, L1_gnn_conv_bias, L1_gnn_bn_gamma, L1_gnn_bn_beta, L1_gnn_w_out, L1_gnn_b_out, L1_gnn_ln_gamma, L1_gnn_ln_beta):
    import jax
    import jax.numpy as jnp

    def _L0_gnn_ref(x, edge_index, edge_type, edge_type_weights, wq, bq, wk, bk, wv, bv, wiq, biq, wik, bik, wiv, biv, wo, bo):
        import jax, jax.numpy as jnp
        import numpy as np
        N = 96
        E = 3072
        IN_F = 1024
        OUT_F = 1024
        H = 16
        D = OUT_F // H
        NUM_ETYPES = 4

        def _build_mask(edge_index, edge_type, edge_type_weights, dtype):
            src, dst = (edge_index[0], edge_index[1])
            w = jax.nn.softplus(edge_type_weights)
            mask = jnp.full((N, N), -jnp.inf, dtype=dtype)
            mask = mask.at[src, dst].set(w[edge_type - 1])
            diag = jnp.diagonal(mask)
            idx = jnp.arange(N)
            mask = mask.at[idx, idx].set(jnp.where(jnp.isneginf(diag), w[3], diag))
            return mask
        q = x @ wq.T + bq
        k = x @ wk.T + bk
        v = x @ wv.T + bv
        q2 = (q @ wiq.T + biq).reshape(N, H, D).transpose(1, 0, 2)
        k2 = (k @ wik.T + bik).reshape(N, H, D).transpose(1, 0, 2)
        v2 = (v @ wiv.T + biv).reshape(N, H, D).transpose(1, 0, 2)
        mask = _build_mask(edge_index, edge_type, edge_type_weights, x.dtype)
        scale = 1.0 / np.sqrt(D).astype(np.float32)
        scores = jnp.einsum('hnd,hmd->hnm', q2, k2) * scale + mask[None]
        attn = jax.nn.softmax(scores, axis=-1)
        out = jnp.einsum('hnm,hmd->hnd', attn, v2)
        out = out.transpose(1, 0, 2).reshape(N, OUT_F)
        return out @ wo.T + bo

    def _L1_gnn_ref(h_text, edge_index, edge_type, w_in, b_in, basis, comp, root, conv_bias, bn_gamma, bn_beta, w_out, b_out, ln_gamma, ln_beta):
        import jax, jax.numpy as jnp
        import numpy as np
        N = 512
        E = 8192
        HID = 1024
        D = 768
        R = 6
        B = 4
        L = 2
        BN_EPS = 1e-05
        LN_EPS = 1e-05

        def _rgcn_conv(x, src, dst, edge_type, basis, comp, root, bias):
            n = x.shape[0]
            W = jnp.einsum('rb,bio->rio', comp, basis)
            h_all = jnp.einsum('ni,rio->rno', x, W)
            counts = jnp.zeros((R, n), x.dtype).at[edge_type, dst].add(1.0)
            norm = 1.0 / counts[edge_type, dst]
            msg = h_all[edge_type, src] * norm[:, None]
            agg = jax.ops.segment_sum(msg, dst, num_segments=n)
            return agg + x @ root + bias

        def _batchnorm(x, gamma, beta):
            mean = jnp.mean(x, axis=0)
            var = jnp.var(x, axis=0)
            return gamma * (x - mean) * jax.lax.rsqrt(var + BN_EPS) + beta

        def _layernorm(x, gamma, beta):
            mean = jnp.mean(x, axis=-1, keepdims=True)
            var = jnp.var(x, axis=-1, keepdims=True)
            return gamma * (x - mean) * jax.lax.rsqrt(var + LN_EPS) + beta
        src, dst = (edge_index[0], edge_index[1])
        x = jax.nn.relu(h_text @ w_in + b_in)
        for l in range(L):
            h_in = x
            x = _rgcn_conv(x, src, dst, edge_type, basis[l], comp[l], root[l], conv_bias[l])
            x = jax.nn.relu(x)
            x = x + h_in
            x = _batchnorm(x, bn_gamma[l], bn_beta[l])
        h_final = x @ w_out + b_out
        return _layernorm(h_final, ln_gamma, ln_beta)
    edge_index = jnp.stack([src, dst])
    x = _layernorm(x + _L0_gnn_ref(x, edge_index, edge_type_5, L0_gnn_edge_type_weights, L0_gnn_wq, L0_gnn_bq, L0_gnn_wk, L0_gnn_bk, L0_gnn_wv, L0_gnn_bv, L0_gnn_wiq, L0_gnn_biq, L0_gnn_wik, L0_gnn_bik, L0_gnn_wiv, L0_gnn_biv, L0_gnn_wo, L0_gnn_bo), axis=-1)
    x = _layernorm(x + _L1_gnn_ref(x, edge_index, edge_type_6, L1_gnn_w_in, L1_gnn_b_in, L1_gnn_basis, L1_gnn_comp, L1_gnn_root, L1_gnn_conv_bias, L1_gnn_bn_gamma, L1_gnn_bn_beta, L1_gnn_w_out, L1_gnn_b_out, L1_gnn_ln_gamma, L1_gnn_ln_beta), axis=-1)
    return x

_drawn_inputs = setup_inputs


def setup_inputs(seed=0):
    import zlib

    import numpy as np

    out = dict(_drawn_inputs(seed))
    spreads = {'L1_gnn_b_in': (0.0, 0.1),
     'L1_gnn_conv_bias': (0.0, 0.1),
     'L1_gnn_bn_gamma': (1.0, 0.2),
     'L1_gnn_bn_beta': (0.0, 0.1),
     'L1_gnn_b_out': (0.0, 0.1),
     'L1_gnn_ln_gamma': (1.0, 0.2),
     'L1_gnn_ln_beta': (0.0, 0.1)}
    factors = {'L0_gnn_edge_type_weights': 7.297,
     'L0_gnn_wq': 4.168,
     'L0_gnn_bq': 8.0,
     'L0_gnn_wk': 4.049,
     'L0_gnn_bk': 64.0,
     'L0_gnn_bv': 6.438,
     'L0_gnn_wiq': 4.078,
     'L0_gnn_biq': 8.0,
     'L0_gnn_wik': 4.115,
     'L0_gnn_bik': 64.0,
     'L0_gnn_biv': 4.102,
     'L0_gnn_bo': 2.683}
    for name, (base, spread) in spreads.items():
        noise = np.random.default_rng([zlib.crc32(name.encode()), seed]).standard_normal(out[name].shape)
        drawn = base * np.exp(spread * noise) if base else spread * noise
        out[name] = jnp.asarray(drawn.astype(out[name].dtype))
    for name, factor in factors.items():
        out[name] = (out[name] * factor).astype(out[name].dtype)
    return out
```

```python
import numpy as np
import concourse.bass as bass
from concourse import mybir
from contextlib import ExitStack

N = 96
E = 1536
F = 1024
HEADS = 16
HD = F // HEADS
D = 768
R = 6
B = 4
L = 2
P = 128
FB = F // P
DB = D // P
ET = E // P
EPS = 1e-5
SCALE = 1.0 / float(np.sqrt(np.float32(HD)))
NEG = -3.0e38

C_BIAS0 = 0
C_BIN = C_BIAS0 + 6 * FB
C_CONV = C_BIN + DB
C_GAMMA = C_CONV + L * DB
C_BETA = C_GAMMA + L * DB
C_COMP = C_BETA + L * DB
C_ETW = C_COMP + L * R * B
NPAR = C_ETW + 4

CODES_AT = 5
CT_AT = 11

SLOTS0 = 2 * FB
SLOTS1 = DB * (1 + B)
PER0, PER1 = 2, 3
WIN_SLOT = SLOTS1 - 9


def gnn_kernel(nc, x, edges, params, rows, w0, wo, w_in, w1, w_out, out):
    f32, bf16, i32 = mybir.dt.float32, mybir.dt.bfloat16, mybir.dt.int32
    ALU, ACT, AX = mybir.AluOpType, mybir.ActivationFunctionType, mybir.AxisListType
    ds = bass.ds

    ctx = ExitStack()
    with ctx:
        def sb(name, cols, dt=f32, parts=P):
            return ctx.enter_context(nc.sbuf_tensor(name, [parts, cols], dt))

        def sem(name):
            return ctx.enter_context(nc.semaphore(name))

        ring0 = sb("ring0", SLOTS0 * F)
        ring1 = sb("ring1", SLOTS1 * D)
        par = sb("par", NPAR)
        rows_sb = sb("rows_sb", F)
        ident = sb("ident", P)
        ones = sb("ones", N)
        x_nat = sb("x_nat", F)
        wT = sb("wT", 2 * F)
        xT_t = sb("xT_t", FB * N)
        hT_t = sb("hT_t", FB * N)
        o2T_t = sb("o2T_t", 3 * FB * N)
        probs = sb("probs", HEADS * N)
        probsT_t = sb("probsT_t", HEADS * N)
        v2n = sb("v2n", F)
        ct = sb("ct", L * B * N)
        mask = sb("mask", N)
        small = sb("small", 256)

        xT = xT_t[:, :].rearrange("p (k n) -> p k n", n=N)
        oT = xT
        hT = hT_t[:, :].rearrange("p (k n) -> p k n", n=N)
        o2T = o2T_t[:, :].rearrange("p (k n) -> p k n", n=N)
        pr = probs[0:N, :].rearrange("p (k c n) -> p k c n", c=4, n=N)
        prT = probsT_t[0:N, :].rearrange("p (k c n) -> p k c n", c=4, n=N)
        r1 = probs[0:N, 0:F]
        x1T = xT
        xn = hT_t[0:N, 0:D]
        cx = o2T_t[:, :].rearrange("p (i b n) -> p i b n", b=B, n=N)
        hxT = probsT_t[:, 0:DB * N].rearrange("p (k n) -> p k n", n=N)
        rT = probsT_t[:, DB * N:2 * DB * N].rearrange("p (k n) -> p k n", n=N)
        gamma_b = wT[0:N, 0:F]
        x1b = wT[0:N, F:2 * F]
        h2 = v2n[0:N, :]
        st = small[:, 0:36].rearrange("p (k s) -> p k s", s=6)
        mv = small[:, 36:48].rearrange("p (k s) -> p k s", s=2)
        std = small[:, 48:54]
        rstd = small[:, 54:60]
        bn_a = small[:, 60:66]
        bn_c = small[:, 66:72]
        bn_m = small[:, 72:78]
        mx = small[:, 80:96].rearrange("p (k c) -> p k c", c=4)
        sm = small[:, 96:112].rearrange("p (k c) -> p k c", c=4)
        rs = small[:, 112:128].rearrange("p (k c) -> p k c", c=4)
        w4 = small[:, 128:132]
        w4n = small[:, 132:136]
        w4e = small[:, 136:140]
        w4l = small[:, 140:144]
        dummy = small[:, 144:145]
        eps = small[:, 145:146]

        at = [0]

        def early(cols, dt=f32):
            words = cols if dt in (f32, i32) else (cols + 1) // 2
            view = ring1[:, at[0]:at[0] + words]
            at[0] += words
            return view if dt == f32 else view.bitcast(dt)

        keyrow = early(E)
        TRI = [P * t * (t + 1) // 2 for t in range(ET + 1)]
        later = early(TRI[ET], bf16)
        S = early(ET * N, bf16).rearrange("p (t n) -> p t n", n=N)
        Dh = early(ET * N, bf16).rearrange("p (t n) -> p t n", n=N)
        Dw = early(ET * N, bf16).rearrange("p (t n) -> p t n", n=N)
        S6 = early(ET * R * N, bf16).rearrange("p (t n) -> p t n", n=R * N)
        diag = early(R * L * B * N)
        nT = early(R * N)
        iota_f = early(R * N)
        iota_i = early(R * N, i32)
        erow_i = early(E, i32)[0:2, :]
        erow = early(E, bf16)[0:2, :]
        ecols_i = early(P, i32)[0:4 * ET, :]
        ecols_f = early(P)[0:4 * ET, :]
        ecol = early(4 * ET)
        keycol = early(ET)
        relcol = early(ET)
        code = early(ET)
        code4 = early(ET)
        dupcode = early(ET)
        counts = early(R)
        rcount = early(R)
        coef = early(L * R * B)
        keyw = early(P, bf16)[0:2, :]
        ones_bf = early(2, bf16)[:, 0:1]
        mcode = early(N)
        mtmp = early(N)
        mtmp2 = early(N)
        assert at[0] <= SLOTS1 * D

        ps = ctx.enter_context(nc.psum_tensor("ps", [P, 8, 512], f32))
        TR = [(0, 1), (2, 3)]
        ACC = (4, 5)
        OUT = (6, 7)
        CX = (2, 3, 6, 7)

        def quad(bank, width=N):
            return ps[:, bank, 0:4 * width].rearrange("p (c n) -> p c n", n=width)

        x_loaded, edges_loaded, erows_loaded = sem("x_loaded"), sem("edges_loaded"), sem("erows_loaded")
        par_loaded, rows_loaded = sem("par_loaded"), sem("rows_loaded")
        w0_loaded = [sem(f"w0_loaded{g}") for g in range(SLOTS0 // PER0)]
        win_loaded = [sem(f"win_loaded{g}") for g in range(2)]
        w1_loaded = [sem(f"w1_loaded{g}") for g in range(SLOTS1 // PER1)]
        wout_loaded = [sem(f"wout_loaded{g}") for g in range(3)]
        stored = [sem(f"stored{h}") for h in range(2)]
        consts_ready = sem("consts_ready")
        keyw_ready = sem("keyw_ready")
        erows_ready = sem("erows_ready")
        keys_spread = sem("keys_spread")
        keys_copied = sem("keys_copied")
        keys_ready = sem("keys_ready")
        turned = sem("turned")
        left_ready = sem("left_ready")
        right_ready = sem("right_ready")
        product = sem("product")
        block_ready = sem("block_ready")
        eq_ready, onehot_ready = sem("eq_ready"), sem("onehot_ready")
        dups_done, hist_done = sem("dups_done"), sem("hist_done")
        dupcode_ready, dw_ready = sem("dupcode_ready"), sem("dw_ready")
        hist_copied, counts_ready, diag_ready = sem("hist_copied"), sem("counts_ready"), sem("diag_ready")
        codes_done, codes_copied, mask_ready = sem("codes_done"), sem("codes_copied"), sem("mask_ready")
        ct_done, ct_ready = sem("ct_done"), sem("ct_ready")
        w4_exp, w4_abs, w4_log, w4_ready = sem("w4_exp"), sem("w4_abs"), sem("w4_log"), sem("w4_ready")
        scored = sem("scored")
        shifted = sem("shifted")
        expd = sem("expd")
        recips = sem("recips")
        probs_ready = sem("probs_ready")
        mixed = sem("mixed")
        oT_ready = sem("oT_ready")
        attended = sem("attended")
        row_spread = sem("row_spread")
        row_copied = sem("row_copied")
        var_ready, std_ready = sem("var_ready"), sem("std_ready")
        x1_ready = sem("x1_ready")
        x1b_ready = sem("x1b_ready")
        in_done = sem("in_done")
        hx_ready = sem("hx_ready")
        rowed = sem("rowed")
        xn_ready = sem("xn_ready")
        cx_done = sem("cx_done")
        cx_even, cx_odd = sem("cx_even"), sem("cx_odd")
        w1_used = sem("w1_used")
        conv_done = sem("conv_done")
        relu_ready = sem("relu_ready")
        out_done = sem("out_done")
        y_ready = sem("y_ready")
        dve_step, pool_step = sem("dve_step"), sem("pool_step")

        w0_v = w0.rearrange("s (t k p) n -> s t p k n", k=PER0, p=P)
        wo_v = wo.rearrange("(t k p) n -> t p k n", k=PER0, p=P)
        win_v = w_in.rearrange("(t k p) n -> t p k n", k=FB // 2, p=P)
        w1_v = w1.rearrange("l (t k p) n -> l t p k n", k=PER1, p=P)
        wout_v = w_out.rearrange("(t k p) n -> t p k n", k=2, p=P)
        slot0 = ring0[:, :].rearrange("p (s n) -> p s n", n=F)
        slot1 = ring1[:, :].rearrange("p (s n) -> p s n", n=D)
        PRE = 1 + 3 * SLOTS0
        WO_T = SLOTS0 // 2

        block = ctx.enter_context(nc.Block())

        @block.sync
        def _(sp):
            sp.dma_start(x_nat[0:N, :], x).then_inc(x_loaded, 16)
            for g in range(SLOTS0 // PER0):
                sp.dma_start(slot0[:, PER0 * g:PER0 * (g + 1), :], w0_v[0, g]).then_inc(w0_loaded[g], 16)
            with sp.Fori(1, 3) as s:
                for g in range(SLOTS0 // PER0):
                    sp.wait_ge(turned, (s - 1) * SLOTS0 + PER0 * (g + 1) + 1)
                    sp.dma_start(slot0[:, PER0 * g:PER0 * (g + 1), :],
                                 w0_v[ds(s, 1), g].rearrange("a p k n -> (a p) k n")).then_inc(w0_loaded[g], 16)
            for g in range(FB // PER0):
                sp.wait_ge(turned, 2 * SLOTS0 + PER0 * (g + 1) + 1)
                sp.dma_start(slot0[:, PER0 * g:PER0 * (g + 1), :], wo_v[g]).then_inc(w0_loaded[g], 16)
            sp.wait_ge(ct_ready, 2)
            sp.wait_ge(mask_ready, 1)
            for h in range(2):
                sp.dma_start(slot1[:, WIN_SLOT + h * (FB // 2):WIN_SLOT + (h + 1) * (FB // 2), :],
                             win_v[h]).then_inc(win_loaded[h], 16)
            for l in range(L):
                for g in range(SLOTS1 // PER1):
                    if l == 0 and g == WIN_SLOT // PER1:
                        sp.wait_ge(in_done, 2)
                    if l > 0 and g < SLOTS1 // PER1 - 1:
                        sp.wait_ge(w1_used, g + 1)
                    elif l > 0:
                        sp.wait_ge(conv_done, 2)
                    sp.dma_start(slot1[:, PER1 * g:PER1 * (g + 1), :], w1_v[l, g]).then_inc(w1_loaded[g], 16)
                if l == 0:
                    sp.wait_ge(turned, PRE + FB)
                    for g in range(3):
                        sp.dma_start(slot0[:, 2 * g:2 * g + 2, :], wout_v[g]).then_inc(wout_loaded[g], 16)
            for h in range(2):
                sp.wait_ge(y_ready, h + 1)
                sp.dma_start(out[:, 512 * h:512 * (h + 1)], probs[0:N, 512 * h:512 * (h + 1)]).then_inc(stored[h], 16)
            for h in range(2):
                sp.wait_ge(stored[h], 16)

        @block.gpsimd
        def _(pool):
            steps = [0]

            def step(ins):
                steps[0] += 1
                ins.then_inc(pool_step, 1)
                pool.wait_ge(pool_step, steps[0])

            step(pool.memset(ident[:, :], 0.0))
            pool.affine_select(out=ident[:, :], in_=ident[:, :], compare_op=ALU.not_equal, fill=1.0, base=0,
                               pattern=[[-1, P]], channel_multiplier=1).then_inc(consts_ready, 1)
            pool.memset(ones[:, :], 1.0).then_inc(consts_ready, 1)
            pool.memset(ones_bf, 1.0).then_inc(consts_ready, 1)
            step(pool.memset(keyw, 1.0))
            pool.memset(keyw[0:1, :], float(N)).then_inc(keyw_ready, 1)
            step(pool.iota(iota_i, [[1, R * N]], base=0, channel_multiplier=0))
            step(pool.tensor_copy(iota_f, iota_i))
            pool.wait_ge(keys_ready, 1)
            pool.wait_ge(keys_copied, 3)
            for hot, col in ((Dh, ecol[:, ET:2 * ET]), (S, ecol[:, 0:ET])):
                for t in range(ET):
                    last = pool.tensor_scalar(hot[:, t, :], iota_f[:, 0:N], col[:, t:t + 1], None, ALU.is_equal)
                last.then_inc(onehot_ready, 1)
            for t in range(ET):
                step(pool.tensor_scalar(later[:, TRI[t]:TRI[t + 1]], keyrow[:, 0:P * (t + 1)],
                                        keycol[:, t:t + 1], None, ALU.is_equal))
                own = later[:, TRI[t + 1] - P:TRI[t + 1]]
                pool.affine_select(out=own, in_=own, compare_op=ALU.is_gt, fill=0.0, base=0,
                                   pattern=[[-1, P]], channel_multiplier=1).then_inc(eq_ready, 1)
            for t in range(ET):
                last = pool.tensor_scalar(S6[:, t, :], iota_f, relcol[:, t:t + 1], None, ALU.is_equal)
            last.then_inc(onehot_ready, 1)
            pool.wait_ge(dupcode_ready, 1)
            pool.tensor_tensor(Dw, Dh, dupcode.unsqueeze(2).to_broadcast([P, ET, N]), ALU.mult).then_inc(dw_ready, 1)
            pool.wait_ge(codes_copied, 1)
            pool.wait_ge(w4_ready, 1)
            step(pool.tensor_scalar(mtmp[0:N, :], mcode[0:N, :], 0.0, 4.0, ALU.is_equal, ALU.mult))
            step(pool.tensor_tensor(mtmp[0:N, :], mtmp[0:N, :], ident[0:N, 0:N], ALU.mult))
            step(pool.tensor_tensor(mcode[0:N, :], mcode[0:N, :], mtmp[0:N, :], ALU.add))
            step(pool.tensor_scalar(mask[0:N, :], mcode[0:N, :], 0.0, NEG, ALU.is_equal, ALU.mult))
            for k in range(4):
                step(pool.tensor_scalar(mtmp2[0:N, :], mcode[0:N, :], float(k + 1), w4[0:N, k:k + 1],
                                        ALU.is_equal, ALU.mult))
                last = pool.tensor_tensor(mask[0:N, :], mask[0:N, :], mtmp2[0:N, :], ALU.add)
                if k < 3:
                    step(last)
            last.then_inc(mask_ready, 1)
            pool.wait_ge(counts_ready, 1)
            step(pool.tensor_tensor(coef[0:N, :].rearrange("p (l r b) -> p l r b", l=L, r=R),
                                    par[0:N, C_COMP:C_COMP + L * R * B].rearrange("p (l r b) -> p l r b", l=L, r=R),
                                    rcount[0:N, :].unsqueeze(1).unsqueeze(3).to_broadcast([N, L, R, B]), ALU.mult))
            diag_v = diag[0:N, :].rearrange("p (r l b n) -> p r l b n", r=R, l=L, b=B)
            coef_v = coef[0:N, :].rearrange("p (l r b) -> p r l b", l=L, r=R)
            for r in range(R):
                pool.tensor_tensor(diag_v[:, r], ident[0:N, 0:N].unsqueeze(1).unsqueeze(1).to_broadcast([N, L, B, N]),
                                   coef_v[:, r].unsqueeze(3).to_broadcast([N, L, B, N]), ALU.mult).then_inc(diag_ready, 1)
            for k in range(4):
                pool.wait_ge(recips, k + 1)
                pool.tensor_tensor(pr[:, k], pr[:, k], rs[0:N, k].unsqueeze(2).to_broadcast([N, 4, N]),
                                   ALU.mult).then_inc(probs_ready, 1)
            pool.wait_ge(row_copied, 4)
            pool.wait_ge(x1_ready, 2)
            pool.tensor_tensor(x1b, x1b, x_nat[0:N, :], ALU.add).then_inc(x1b_ready, 1)


        @block.scalar
        def _(act):
            act.dma_start(ecols_i, edges.rearrange("a (t p) -> (a t) p", p=P)).then_inc(edges_loaded, 16)
            act.dma_start(erow_i, edges[0:2, :]).then_inc(erows_loaded, 16)
            act.dma_start(par[:, :], params).then_inc(par_loaded, 16)
            for k in range(4):
                act.dma_start(rows_sb[32 * k:32 * k + 1, :], rows[k:k + 1, :]).then_inc(rows_loaded, 16)
            act.wait_ge(turned, 1)
            act.activation(xT[:, 0:4, :], quad(0), ACT.Copy).then_inc(left_ready, 1)
            act.wait_ge(keys_spread, 1)
            for c in range(2):
                act.activation(keyrow[:, 512 * c:512 * (c + 1)], ps[:, 5 + c, :], ACT.Copy).then_inc(keys_copied, 1)

            def left(batch, j):
                act.wait_ge(turned, batch + 1)
                act.activation(wT[:, F * (j % 2):F * (j % 2) + 512], ps[:, TR[j % 2][0], :],
                               ACT.Copy).then_inc(left_ready, 1)

            left(1, 0)
            act.wait_ge(w4_abs, 1)
            act.activation(w4e, w4n, ACT.Exp).then_inc(w4_exp, 1)
            act.wait_ge(w4_exp, 1)
            act.activation(w4l, w4e, ACT.Ln, bias=1.0).then_inc(w4_log, 1)
            with act.Fori(0, 2) as s:
                for j in range(SLOTS0):
                    act.wait_ge(product, s * SLOTS0 + (j + 1))
                    left(s * SLOTS0 + (j + 2), j + 1)
            for j in range(SLOTS0):
                act.wait_ge(product, 2 * SLOTS0 + j + 1)
                left(2 * SLOTS0 + j + 2, j + 1)
                if j == CT_AT:
                    act.wait_ge(ct_done, 1)
                    act.activation(ct[0:N, 0:B * N], ps[0:N, OUT[0], 0:B * N], ACT.Copy).then_inc(ct_ready, 1)
            for m in range(1, FB + 1):
                act.wait_ge(turned, PRE + m + 1)
                act.activation(slot0[:, WO_T + m, 0:512] if m < FB else v2n[0:N, 0:512],
                               ps[0:P if m < FB else N, TR[m % 2][0], :], ACT.Copy).then_inc(left_ready, 1)
                if 2 <= m < 6:
                    act.wait_ge(shifted, m - 1)
                    act.activation(pr[:, m - 2], pr[:, m - 2], ACT.Exp).then_inc(expd, 1)
            act.activation(dummy, ident[:, 0:1], ACT.Sqrt)
            for h in range(2):
                act.wait_ge(turned, PRE + FB + h + 2)
                act.activation(prT[:, 2 * h], quad(TR[1 - h][0])[0:N], ACT.Copy).then_inc(left_ready, 1)
            act.wait_ge(mixed, 1)
            act.activation(oT[:, 0:4, :], quad(ACC[0]), ACT.Copy).then_inc(oT_ready, 1)
            for k in range(2):
                for h in range(2):
                    act.wait_ge(row_spread, 2 * k + h + 1)
                    act.activation(wT[0:N, F * k + 512 * h:F * k + 512 * (h + 1)],
                                   ps[0:N, (ACC, TR[0])[k][h], :], ACT.Copy).then_inc(row_copied, 1)
            act.wait_ge(var_ready, 1)
            act.activation(std[0:N, 0:1], mv[0:N, 0, 1:2], ACT.Sqrt, bias=eps[0:N, :]).then_inc(std_ready, 1)
            act.wait_ge(turned, PRE + FB + 4)
            act.activation(x1T[:, 0:4, :], quad(TR[1][0]), ACT.Copy).then_inc(left_ready, 1)
            with act.Fori(0, L) as l:
                act.wait_ge(rowed, 2 * l + 1)
                act.activation(xn[:, 0:512], ps[0:N, TR[0][0], :], ACT.Copy).then_inc(xn_ready, 1)
                for i in range(0, DB, 2):
                    act.wait_ge(cx_done, l * DB + i + 1)
                    act.activation(cx[:, i], quad(CX[i % 4]), ACT.Copy).then_inc(cx_even, 1)
                for o in range(DB):
                    if o % 3 == 0:
                        act.wait_ge(conv_done, 2 * l + o // 3 + 1)
                    act.activation(rT[:, o, :], ps[:, ACC[o // 3], N * (o % 3):N * (o % 3 + 1)], ACT.Relu,
                                   bias=par[:, ds(l * DB + (C_CONV + o), 1)]).then_inc(relu_ready, 1)
                act.wait_ge(var_ready, l + 2)
                act.activation(std, mv[:, 0:DB, 1], ACT.Sqrt, bias=eps).then_inc(std_ready, 1)
            for k in range(2):
                act.wait_ge(var_ready, L + 2 + k)
                act.activation(std[0:N, 0:1], mv[0:N, 0, 1:2], ACT.Sqrt, bias=eps[0:N, :]).then_inc(std_ready, 1)

        @block.vector
        def _(dve):
            steps = [0, 0]

            def step(ins):
                steps[1] += 1
                ins.then_inc(dve_step, 1)
                dve.wait_ge(dve_step, steps[0] + steps[1])

            dve.memset(eps, EPS).then_inc(consts_ready, 1)
            dve.wait_ge(edges_loaded, 16)
            dve.tensor_copy(ecols_f, ecols_i).then_inc(erows_ready, 1)
            dve.wait_ge(erows_loaded, 16)
            dve.tensor_copy(erow, erow_i).then_inc(erows_ready, 1)
            dve.wait_ge(turned, 1)
            dve.tensor_copy(xT[:, 4:8, :], quad(1)).then_inc(right_ready, 1)
            dve.wait_ge(keys_spread, 1)
            dve.wait_ge(product, 1)
            dve.tensor_copy(ecol, ps[:, 4, 0:4 * ET]).then_inc(block_ready, 1)
            dve.wait_ge(block_ready, 1)
            dve.tensor_copy(keyrow[:, 1024:1536], ps[:, 7, :]).then_inc(keys_copied, 1)
            src, dst = ecol[:, 0:ET], ecol[:, ET:2 * ET]
            typ5, typ6 = ecol[:, 2 * ET:3 * ET], ecol[:, 3 * ET:4 * ET]
            step(dve.tensor_scalar(code4, typ5, 0.0, 4.0, ALU.is_equal, ALU.mult))
            dve.tensor_tensor(code, code4, typ5, ALU.add)
            dve.scalar_tensor_tensor(relcol, typ6, float(N), src, ALU.mult, ALU.add)
            dve.scalar_tensor_tensor(keycol, src, float(N), dst, ALU.mult, ALU.add).then_inc(keys_ready, 1)

            def right(batch, j):
                dve.wait_ge(turned, batch + 1)
                dve.tensor_copy(wT[:, F * (j % 2) + 512:F * (j % 2) + 1024],
                                ps[:, TR[j % 2][1], :]).then_inc(right_ready, 1)

            def pair(s):
                base = s * SLOTS0 + 1
                for j in range(SLOTS0):
                    dve.wait_ge(product, base + j)
                    right(base + j + 1, j + 1)
                    dve.wait_ge(product, base + j + 1)
                    dst = hT[:, j, :] if j < FB else o2T[:, ds(s * FB + (j - FB), 1), :].squeeze(1)
                    dve.tensor_scalar(dst, ps[:, ACC[j % 2], 0:N], par[:, ds(s * SLOTS0 + (C_BIAS0 + j), 1)],
                                      None, ALU.add).then_inc(block_ready, 1)
                    yield j

            right(1, 0)
            dve.wait_ge(par_loaded, 16)
            etw = par[:, C_ETW:C_ETW + 4]
            step(dve.tensor_scalar(w4n, etw, -1.0, None, ALU.mult))
            dve.tensor_tensor(w4n, w4n, etw, ALU.min).then_inc(w4_abs, 1)
            dve.wait_ge(w4_log, 1)
            dve.scalar_tensor_tensor(w4, etw, 0.0, w4l, ALU.max, ALU.add).then_inc(w4_ready, 1)
            with dve.Fori(0, 2) as s:
                for _ in pair(s):
                    pass
            dve.wait_ge(dups_done, 1)
            dve.scalar_tensor_tensor(dupcode, ps[:, OUT[0], 0:ET], 0.0, code, ALU.is_equal,
                                     ALU.mult).then_inc(dupcode_ready, 1)
            dve.wait_ge(hist_done, 1)
            dve.tensor_copy(nT[0:N, 0:288], ps[0:N, OUT[1], 0:288]).then_inc(hist_copied, 1)
            for j in pair(2):
                if j == CODES_AT:
                    dve.wait_ge(codes_done, 1)
                    dve.tensor_copy(mcode[0:N, :], ps[0:N, OUT[0], 0:N]).then_inc(codes_copied, 1)
                    dve.wait_ge(hist_done, 2)
                    step(dve.tensor_copy(nT[0:N, 288:576], ps[0:N, OUT[1], 0:288]))
                    step(dve.tensor_reduce(counts[0:N, :], nT[0:N, :].rearrange("p (r n) -> p r n", n=N),
                                           AX.X, ALU.add))
                    step(dve.tensor_scalar(counts[0:N, :], counts[0:N, :], 1.0, None, ALU.max))
                    dve.reciprocal(rcount[0:N, :], counts[0:N, :]).then_inc(counts_ready, 1)
                if j == CT_AT:
                    dve.wait_ge(ct_done, 2)
                    dve.tensor_copy(ct[0:N, B * N:2 * B * N], ps[0:N, OUT[1], 0:B * N]).then_inc(ct_ready, 1)

            def shift(k):
                dve.wait_ge(scored, k + 1)
                step(dve.scalar_tensor_tensor(pr[:, k], quad(4 + k)[0:N], SCALE,
                                              mask[0:N, :].unsqueeze(1).to_broadcast([N, 4, N]), ALU.mult, ALU.add))
                step(dve.tensor_reduce(mx[0:N, k], pr[:, k], AX.X, ALU.max))
                dve.tensor_tensor(pr[:, k], pr[:, k], mx[0:N, k].unsqueeze(2).to_broadcast([N, 4, N]),
                                  ALU.subtract).then_inc(shifted, 1)

            def total(k):
                dve.wait_ge(expd, k + 1)
                step(dve.tensor_reduce(sm[0:N, k], pr[:, k], AX.X, ALU.add))
                dve.reciprocal(rs[0:N, k], sm[0:N, k]).then_inc(recips, 1)

            dve.wait_ge(mask_ready, 1)
            for m in range(1, FB + 1):
                if m <= 4:
                    shift(m - 1)
                dve.wait_ge(turned, PRE + m + 1)
                dve.tensor_copy(slot0[:, WO_T + m, 512:1024] if m < FB else v2n[0:N, 512:1024],
                                ps[0:P if m < FB else N, TR[m % 2][1], :]).then_inc(right_ready, 1)
                if m > 4:
                    total(m - 5)
            for h in range(2):
                dve.wait_ge(turned, PRE + FB + h + 2)
                dve.tensor_copy(prT[:, 2 * h + 1], quad(TR[1 - h][1])[0:N]).then_inc(right_ready, 1)
            dve.wait_ge(mixed, 2)
            dve.tensor_copy(oT[:, 4:8, :], quad(ACC[1])).then_inc(oT_ready, 1)

            def mean_var(v):
                dve.bn_aggr(mv[0:N, 0, :], st[0:N, 0:2, :]).then_inc(var_ready, 1)
                dve.wait_ge(std_ready, v)
                step(dve.reciprocal(rstd[0:N, 0:1], std[0:N, 0:1]))

            for h in range(2):
                half = slice(512 * h, 512 * (h + 1))
                dve.wait_ge(attended, h + 1)
                step(dve.tensor_tensor(r1[:, half], ps[0:N, OUT[h], :], x_nat[0:N, half], ALU.add))
                step(dve.bn_stats(st[0:N, h, :], r1[:, half]))
            mean_var(1)
            for h in range(2):
                half = slice(512 * h, 512 * (h + 1))
                dve.tensor_scalar(x_nat[0:N, half], r1[:, half], mv[0:N, 0, 0:1], rstd[0:N, 0:1],
                                  ALU.subtract, ALU.mult).then_inc(x1_ready, 1)
            dve.wait_ge(turned, PRE + FB + 4)
            dve.tensor_copy(x1T[:, 4:8, :], quad(TR[1][1])).then_inc(right_ready, 1)
            for o in range(DB):
                if o % 3 == 0:
                    dve.wait_ge(in_done, o // 3 + 1)
                dve.tensor_scalar(hxT[:, o, :], ps[:, ACC[o // 3], N * (o % 3):N * (o % 3 + 1)],
                                  par[:, C_BIN + o:C_BIN + o + 1], 0.0, ALU.add, ALU.max).then_inc(hx_ready, 1)
            before = steps[1]
            with dve.Fori(0, L) as l:
                steps[0] = l * (2 + DB + 4)
                dve.wait_ge(rowed, 2 * l + 2)
                dve.tensor_copy(xn[:, 512:768], ps[0:N, TR[0][1], 0:256]).then_inc(xn_ready, 1)
                for i in range(1, DB, 2):
                    dve.wait_ge(cx_done, l * DB + i + 1)
                    dve.tensor_copy(cx[:, i], quad(CX[i % 4])).then_inc(cx_odd, 1)
                for h in range(2):
                    dve.wait_ge(relu_ready, l * DB + 3 * (h + 1))
                    step(dve.tensor_tensor(rT[:, 3 * h:3 * h + 3, :], rT[:, 3 * h:3 * h + 3, :],
                                           hxT[:, 3 * h:3 * h + 3, :], ALU.add))
                    for o in range(3 * h, 3 * h + 3):
                        steps[1] += 1
                        dve.bn_stats(st[:, o, :], rT[:, o, :]).then_inc(dve_step, 1)
                dve.wait_ge(dve_step, steps[0] + steps[1])
                dve.memset(bn_m, 0.0)
                for o in range(DB):
                    aggr = dve.bn_aggr(mv[:, o, :], st[:, o, :])
                aggr.then_inc(var_ready, 1)
                dve.wait_ge(std_ready, l + 2)
                step(dve.reciprocal(rstd, std))
                step(dve.tensor_tensor(bn_a, rstd, par[:, ds(l * DB + C_GAMMA, DB)], ALU.mult))
                step(dve.tensor_tensor(bn_m, mv[:, 0:DB, 0], bn_a, ALU.mult))
                step(dve.tensor_tensor(bn_c, par[:, ds(l * DB + C_BETA, DB)], bn_m, ALU.subtract))
                for o in range(DB):
                    dve.tensor_scalar(hxT[:, o, :], rT[:, o, :], bn_a[:, o:o + 1], bn_c[:, o:o + 1],
                                      ALU.mult, ALU.add).then_inc(hx_ready, 1)
            assert steps[1] - before == 2 + DB + 4
            steps[:] = [0, before + L * (2 + DB + 4)]
            for h in range(2):
                dve.wait_ge(out_done, h + 1)
                step(dve.bn_stats(st[0:N, h, :], ps[0:N, OUT[h], :]))
            mean_var(L + 2)
            dve.wait_ge(x1b_ready, 1)
            for h in range(2):
                half = slice(512 * h, 512 * (h + 1))
                step(dve.scalar_tensor_tensor(h2[:, half], ps[0:N, OUT[h], :], mv[0:N, 0, 0:1], gamma_b[:, half],
                                              ALU.subtract, ALU.mult))
                step(dve.scalar_tensor_tensor(h2[:, half], h2[:, half], rstd[0:N, 0:1], x1b[:, half],
                                              ALU.mult, ALU.add))
                step(dve.bn_stats(st[0:N, h, :], h2[:, half]))
            mean_var(L + 3)
            for h in range(2):
                half = slice(512 * h, 512 * (h + 1))
                dve.tensor_scalar(probs[0:N, half], h2[:, half], mv[0:N, 0, 0:1], rstd[0:N, 0:1],
                                  ALU.subtract, ALU.mult).then_inc(y_ready, 1)

        @block.tensor
        def _(pe):
            pe.wait_ge(consts_ready, 4)
            pe.wait_ge(x_loaded, 16)
            for i in range(FB):
                last = pe.transpose(quad(i // 4)[:, i % 4], x_nat[0:N, P * i:P * (i + 1)], ident[0:N, 0:N])
            last.then_inc(turned, 1)
            pe.wait_ge(erows_ready, 2)
            pe.wait_ge(keyw_ready, 1)
            pe.transpose(ps[:, 4, 0:4 * ET], ecols_f, ident[0:4 * ET, 0:4 * ET]).then_inc(product, 1)
            for c in range(3):
                last = pe.matmul(ps[:, 5 + c, :], keyw, erow[:, 512 * c:512 * (c + 1)], start=True, stop=True)
            last.then_inc(keys_spread, 1)

            def turn(slot, buf):
                for i in range(FB):
                    last = pe.transpose(ps[:, TR[buf][i // 4], P * (i % 4):P * (i % 4 + 1)],
                                        slot0[:, slot, P * i:P * (i + 1)], ident[:, :])
                last.then_inc(turned, 1)

            def pair(s):
                base = s * SLOTS0 + 1
                for j in range(SLOTS0):
                    slot = (j + 1) % SLOTS0
                    if slot % PER0 == 0:
                        pe.wait_ge(w0_loaded[slot // PER0], 16 * s + (16 if slot else 32))
                    pe.wait_ge(left_ready, base + j)
                    pe.wait_ge(right_ready, base + j)
                    turn(slot, (j + 1) % 2)
                    pe.wait_ge(left_ready, base + j + 1)
                    pe.wait_ge(right_ready, base + j + 1)
                    pe.wait_ge(block_ready, base + j)
                    rhs = xT if j < FB else hT
                    for i in range(FB):
                        last = pe.matmul(ps[:, ACC[j % 2], 0:N], wT[:, F * (j % 2) + P * i:F * (j % 2) + P * (i + 1)],
                                         rhs[:, i, :], start=(i == 0), stop=(i == FB - 1))
                    last.then_inc(product, 1)
                    yield j

            pe.wait_ge(left_ready, 1)
            pe.wait_ge(right_ready, 1)
            pe.wait_ge(w0_loaded[0], 16)
            turn(0, 0)
            pe.wait_ge(keys_copied, 3)
            with pe.Fori(0, 2) as s:
                for _ in pair(s):
                    pass
            pe.wait_ge(eq_ready, ET)
            for t in range(ET):
                for u in range(t, ET):
                    last = pe.matmul(ps[:, OUT[0], t:t + 1], later[:, TRI[u] + P * t:TRI[u] + P * (t + 1)], ones_bf,
                                     start=(u == t), stop=(u == ET - 1))
            last.then_inc(dups_done, 1)

            def hist(h):
                for t in range(ET):
                    last = pe.matmul(ps[0:N, OUT[1], 0:288], Dh[:, t, :], S6[:, t, 288 * h:288 * (h + 1)],
                                     start=(t == 0), stop=(t == ET - 1))
                last.then_inc(hist_done, 1)

            pe.wait_ge(onehot_ready, 3)
            hist(0)
            for j in pair(2):
                if j == CODES_AT:
                    pe.wait_ge(dw_ready, 1)
                    for t in range(ET):
                        last = pe.matmul(ps[0:N, OUT[0], 0:N], S[:, t, :], Dw[:, t, :],
                                         start=(t == 0), stop=(t == ET - 1))
                    last.then_inc(codes_done, 1)
                    pe.wait_ge(hist_copied, 1)
                    hist(1)
                if j == CT_AT:
                    pe.wait_ge(diag_ready, R)
                    pe.wait_ge(codes_copied, 1)
                    for l in range(L):
                        for r in range(R):
                            last = pe.matmul(ps[0:N, OUT[l], 0:B * N], nT[0:N, N * r:N * (r + 1)],
                                             diag[0:N, (r * L + l) * B * N:(r * L + l + 1) * B * N],
                                             start=(r == 0), stop=(r == R - 1))
                        last.then_inc(ct_done, 1)
            pe.wait_ge(block_ready, 3 * SLOTS0 + 1)
            for half in range(2):
                if half == 1:
                    pe.wait_ge(ct_ready, 2)
                for c in range(4):
                    for odd in range(2):
                        hd = slice(HD * odd, HD * (odd + 1))
                        blk = 4 * half + c
                        last = pe.matmul(quad(4 + 2 * half + odd)[0:N, c], o2T[hd, FB + blk, :],
                                         o2T[hd, 2 * FB + blk, :], start=True, stop=True)
                        if c == 3:
                            last.then_inc(scored, 1)
            for m in range(1, FB + 1):
                if m < FB and m % PER0 == 0:
                    pe.wait_ge(w0_loaded[m // PER0], 16 * 4)
                pe.wait_ge(left_ready, PRE + m - 1)
                pe.wait_ge(right_ready, PRE + m - 1)
                if m < FB:
                    turn(m, m % 2)
                else:
                    for i in range(FB):
                        last = pe.transpose(ps[0:N, TR[0][i // 4], P * (i % 4):P * (i % 4 + 1)], o2T[:, i, :],
                                            ident[:, :])
                    last.then_inc(turned, 1)
            for h in range(2):
                pe.wait_ge(left_ready, PRE + FB + h)
                pe.wait_ge(right_ready, PRE + FB + h)
                pe.wait_ge(probs_ready, 2 * h + 2)
                for k in range(2):
                    for c in range(4):
                        last = pe.transpose(quad(TR[1 - h][k])[0:N, c], pr[:, 2 * h + k, c], ident[0:N, 0:N])
                last.then_inc(turned, 1)
            for h in range(2):
                pe.wait_ge(left_ready, PRE + FB + h + 2)
                pe.wait_ge(right_ready, PRE + FB + h + 2)
                for c in range(4):
                    for odd in range(2):
                        head = 8 * h + 2 * c + odd
                        last = pe.matmul(quad(ACC[h])[HD * odd:HD * (odd + 1), c],
                                         v2n[0:N, HD * head:HD * (head + 1)], prT[:, 2 * h + odd, c],
                                         start=True, stop=True)
                last.then_inc(mixed, 1)
            pe.wait_ge(rows_loaded, 64)

            def seed(row, h, stop=False):
                return pe.matmul(ps[0:N, OUT[h], :], ones[32 * row:32 * row + 1, :],
                                 rows_sb[32 * row:32 * row + 1, 512 * h:512 * (h + 1)],
                                 start=True, stop=stop, skip_group_check=True)

            for h in range(2):
                seed(0, h)
            pe.wait_ge(oT_ready, 2)
            for j in range(FB):
                for i in range(FB):
                    rhs = slot0[:, WO_T + j, P * i:P * (i + 1)] if j else wT[:, P * i:P * (i + 1)]
                    last = pe.matmul(ps[0:N, OUT[j // 4], P * (j % 4):P * (j % 4 + 1)], oT[:, i, :], rhs,
                                     start=False, stop=(i == FB - 1), skip_group_check=True)
                if j % 4 == 3:
                    last.then_inc(attended, 1)
            for k in range(2):
                for h in range(2):
                    row = 2 + k
                    pe.matmul(ps[0:N, (ACC, TR[0])[k][h], :], ones[32 * row:32 * row + 1, :],
                              rows_sb[32 * row:32 * row + 1, 512 * h:512 * (h + 1)],
                              start=True, stop=True).then_inc(row_spread, 1)
            for i in range(FB):
                if i % 4 == 0:
                    pe.wait_ge(x1_ready, i // 4 + 1)
                last = pe.transpose(quad(TR[1][i // 4])[:, i % 4], x_nat[0:N, P * i:P * (i + 1)], ident[0:N, 0:N])
            last.then_inc(turned, 1)
            pe.wait_ge(row_copied, 4)
            for i in range(FB):
                if i % 4 == 0:
                    pe.wait_ge(win_loaded[i // 4], 16)
                    pe.wait_ge((left_ready, right_ready)[i // 4], PRE + FB + 4)
                for o in range(DB):
                    last = pe.matmul(ps[:, ACC[o // 3], N * (o % 3):N * (o % 3 + 1)],
                                     slot1[:, WIN_SLOT + i, P * o:P * (o + 1)], x1T[:, i, :],
                                     start=(i == 0 and o % 3 == 0), stop=(i == FB - 1), skip_group_check=True)
                    if i == FB - 1 and o % 3 == 2:
                        last.then_inc(in_done, 1)
            with pe.Fori(0, L) as l:
                for o in range(DB):
                    pe.wait_ge(hx_ready, l * DB + o + 1)
                    last = pe.transpose(ps[0:N, TR[0][o // 4], P * (o % 4):P * (o % 4 + 1)], hxT[:, o, :], ident[:, :])
                    if o in (3, DB - 1):
                        last.then_inc(rowed, 1)

                def conv(k, rhs):
                    if k % PER1 == 0:
                        pe.wait_ge(w1_loaded[k // PER1], 16 * l + 16)
                    for o in range(DB):
                        last = pe.matmul(ps[:, ACC[o // 3], N * (o % 3):N * (o % 3 + 1)],
                                         slot1[:, k, P * o:P * (o + 1)], rhs,
                                         start=(k == 0 and o % 3 == 0), stop=(k == SLOTS1 - 1), skip_group_check=True)
                        if k == SLOTS1 - 1 and o % 3 == 2:
                            last.then_inc(conv_done, 1)
                    return last

                for i in range(DB):
                    last = conv(i, hxT[:, i, :])
                    if i % PER1 == PER1 - 1:
                        last.then_inc(w1_used, 1)
                pe.wait_ge(xn_ready, 2 * l + 2)
                for i in range(DB):
                    if i >= 4:
                        pe.wait_ge((cx_even, cx_odd)[i % 2], l * (DB // 2) + (i - 4) // 2 + 1)
                    pe.matmul(ps[:, CX[i % 4], 0:B * N], xn[:, P * i:P * (i + 1)],
                              ct[0:N, ds(l * (B * N), B * N)], start=True, stop=True).then_inc(cx_done, 1)
                for b in range(B):
                    for i in range(DB):
                        if b == 0:
                            pe.wait_ge((cx_even, cx_odd)[i % 2], l * (DB // 2) + i // 2 + 1)
                        k = DB * (1 + b) + i
                        last = conv(k, cx[:, i, b, :])
                        if k % PER1 == PER1 - 1 and k < SLOTS1 - 1:
                            last.then_inc(w1_used, 1)
            pe.wait_ge(hx_ready, (L + 1) * DB)
            for h in range(2):
                seed(1, h)
            for i in range(DB):
                if i % 2 == 0:
                    pe.wait_ge(wout_loaded[i // 2], 16)
                for h in range(2):
                    last = pe.matmul(ps[0:N, OUT[h], :], hxT[:, i, :], slot0[:, i, 512 * h:512 * (h + 1)],
                                     start=False, stop=(i == DB - 1), skip_group_check=True)
                    if i == DB - 1:
                        last.then_inc(out_done, 1)


def kernel(**a):
    import concourse.bacc as bacc
    from concourse.bass_utils import run_bass_kernel_spmd

    def flat(name):
        return np.asarray(a[name])

    def cols(*vectors):
        return np.concatenate([v.reshape(-1, P).T for v in vectors], axis=1)

    def spread(v):
        return np.broadcast_to(v.reshape(1, -1), (P, v.size))

    g0, g1 = "L0_gnn_", "L1_gnn_"
    order = ("v", "iv", "q", "iq", "k", "ik")
    arrays = {
        "x": flat("x"),
        "edges": np.stack([flat(n) for n in ("src", "dst", "edge_type_5", "edge_type_6")]),
        "params": np.ascontiguousarray(np.concatenate(
            [cols(*[flat(g0 + "b" + n) for n in order], flat(g1 + "b_in"), flat(g1 + "conv_bias"),
                  flat(g1 + "bn_gamma"), flat(g1 + "bn_beta")),
             spread(flat(g1 + "comp")), spread(flat(g0 + "edge_type_weights"))], axis=1)),
        "rows": np.stack([flat(g0 + "bo"), flat(g1 + "b_out"), flat(g1 + "ln_gamma"), flat(g1 + "ln_beta")]),
        "w0": np.stack([flat(g0 + "w" + n) for n in order]).reshape(3, 2 * F, F),
        "wo": flat(g0 + "wo"),
        "w_in": flat(g1 + "w_in"),
        "w1": np.concatenate([flat(g1 + "root")[:, None], flat(g1 + "basis")], axis=1).reshape(L, (1 + B) * D, D),
        "w_out": flat(g1 + "w_out"),
    }
    nc = bacc.Bacc("TRN2", target_bir_lowering=False, num_devices=1)
    aps = {n: nc.dram_tensor(f"in_{n}", v.shape, mybir.dt.from_np(v.dtype), kind="ExternalInput").ap()
           for n, v in arrays.items()}
    out = nc.dram_tensor("out", (N, F), mybir.dt.float32, kind="ExternalOutput").ap()
    gnn_kernel(nc, out=out, **aps)
    result = run_bass_kernel_spmd(nc, [{f"in_{n}": v for n, v in arrays.items()}], core_ids=[0])
    return result.results[0]["out"]
```

```python
import numpy as np
import concourse.bass as bass
from concourse import mybir
from contextlib import ExitStack

N = 96
E = 1536
F = 1024
HEADS = 16
HD = F // HEADS
D = 768
R = 6
B = 4
L = 2
P = 128
FB = F // P
DB = D // P
ET = E // P
EPS = 1e-5
SCALE = 1.0 / float(np.sqrt(np.float32(HD)))
NEG = -3.0e38

C_BIAS0 = 0
C_BIN = C_BIAS0 + 6 * FB
C_CONV = C_BIN + DB
C_GAMMA = C_CONV + L * DB
C_BETA = C_GAMMA + L * DB
C_COMP = C_BETA + L * DB
C_ETW = C_COMP + L * R * B
NPAR = C_ETW + 4

ORDER = ("q", "k", "iq", "ik", "v", "iv")
Q1, K1, Q2, K2, V1, V2 = range(6)

PROJ = 0
WO = PROJ + 6 * FB
WIN = WO + FB
CONV = WIN + FB
LAYER = DB * (1 + B)
WOUT = CONV + L * LAYER
BLOCKS = WOUT + DB
SLOT = {Q1: 0, K1: 1, V1: 2}
DUPS_AT, ADJ_AT, CNT_AT, CODES_AT = 3, 12, 16, 20
BEHIND = 2
RING = LAYER * D
HALVES = 3


def transfers():
    out = [(n, 2, F, (n // 2 % (RING // (2 * F))) * 2 * F) for n in range(PROJ, WIN, 2)]
    out += [(WIN + 3 * g, min(3, FB - 3 * g), D, (7 + g) * 3 * D) for g in range(3)]
    out += [(n, 3, D, (n - CONV) % LAYER * D) for n in range(CONV, WOUT, 3)]
    return out + [(n, 2, F, (n - WOUT) * F) for n in range(WOUT, BLOCKS, 2)]


def gnn_kernel(nc, x, xt, edges, ecols, params, rows, wp, w_in, wc, w_out, out):
    f32, f32r, bf16, f16 = mybir.dt.float32, mybir.dt.float32r, mybir.dt.bfloat16, mybir.dt.float16
    i32 = mybir.dt.int32
    ALU, ACT, AX = mybir.AluOpType, mybir.ActivationFunctionType, mybir.AxisListType
    ds = bass.ds

    ctx = ExitStack()
    with ctx:
        def sb(name, cols, dt=f32, parts=P):
            return ctx.enter_context(nc.sbuf_tensor(name, [parts, cols], dt))

        def sem(name):
            return ctx.enter_context(nc.semaphore(name))

        ring = sb("ring", RING)
        w_high = sb("w_high", HALVES * F, f32r)
        w_low = sb("w_low", HALVES * F, f32r)
        x_high = sb("x_high", FB * N, f32r)
        x_low = sb("x_low", FB * N, f32r)
        h_high = sb("h_high", DB * B * N, f32r)
        h_low = sb("h_low", DB * B * N, f32r)
        par = sb("par", NPAR)
        rows_sb = sb("rows_sb", F)
        ident = sb("ident", P)
        ones = sb("ones", N)
        x_nat = sb("x_nat", F)
        turnT = sb("turnT", FB * N)
        flat_sb = sb("flat", F)
        work = sb("work", 8960)
        small = sb("small", 512)

        def blocks(view, width=N):
            return view.rearrange("p (k n) -> p k n", n=width)

        xh, xl, turned_v = blocks(x_high[:, :]), blocks(x_low[:, :]), blocks(turnT[:, :])
        cxh = h_high[:, :].rearrange("p (i b n) -> p i b n", b=B, n=N)
        cxl = h_low[:, :].rearrange("p (i b n) -> p i b n", b=B, n=N)
        hh = h_high[:, :].rearrange("p (s k n) -> p s k n", s=3, n=N)
        hl = h_low[:, :].rearrange("p (s k n) -> p s k n", s=3, n=N)
        probs, probsT = work[0:N, 0:1536], work[:, 1536:3072]
        pr = probs.rearrange("p (k c n) -> p k c n", c=4, n=N)
        prT = probsT[0:N, :].rearrange("p (k c n) -> p k c n", c=4, n=N)
        v2 = work[0:N, 3072:4096]
        q2T, k2T = blocks(work[:, 4096:4864]), blocks(work[:, 4864:5632])
        gamma_b, x1b = work[0:N, 5632:6656], work[0:N, 6656:7680]
        ct = work[0:N, 8192:8960]
        r1, y_out = probs[:, 0:F], probs[:, 0:F]
        hx = blocks(probsT[:, 0:DB * N])
        rT = blocks(probsT[:, DB * N:2 * DB * N])
        xn = flat_sb[0:N, 0:D]
        h2 = v2

        erow_i = work[0:2, 0:1536].bitcast(i32)
        erow = work[0:2, 1536:2304].bitcast(bf16)
        D6 = blocks(work[:, 0:3456].bitcast(bf16), R * N)
        S = blocks(work[:, 3456:4032].bitcast(bf16))
        Dh = blocks(work[:, 4032:4608].bitcast(bf16))
        Dw = blocks(work[:, 4608:5184].bitcast(bf16))
        later = blocks(work[:, 5184:5952].bitcast(bf16), P)
        tri = work[:, 5952:6080]
        iota = work[:, 6080:6368].bitcast(f16)
        adj = work[0:N, 6368:6944]
        cnt = work[0:N, 6944:7520]
        term = work[0:N, 7520:7904]
        mcode, mtmp, mbits = (work[0:N, 7904 + N * k:8000 + N * k] for k in range(3))
        msum, mlead = work[0:N, 7520:7616], work[0:N, 7616:7712]
        mask = small[0:N, 400:496]

        st = small[:, 0:36].rearrange("p (k s) -> p k s", s=6)
        mv = small[:, 36:48].rearrange("p (k s) -> p k s", s=2)
        std, rstd = small[:, 48:54], small[:, 54:60]
        bn_a, bn_c, bn_m = small[:, 60:66], small[:, 66:72], small[:, 72:78]
        mx = small[:, 80:96].rearrange("p (k c) -> p k c", c=4)
        sm = small[:, 96:112].rearrange("p (k c) -> p k c", c=4)
        rs = small[:, 112:128].rearrange("p (k c) -> p k c", c=4)
        w4, w4n, w4e, w4l = (small[:, 128 + 4 * k:132 + 4 * k] for k in range(4))
        eps, dummy = small[:, 144:145], small[:, 145:146]
        ones_bf = small[:, 146:147].bitcast(bf16)[:, 0:1]
        keyw = small[0:2, 148:212].bitcast(bf16)
        ecol_i = small[:, 212:260].bitcast(i32)
        ecol = small[:, 260:308]
        src, dst, typ5, typ6 = (ecol[:, ET * k:ET * (k + 1)] for k in range(4))
        keycol, relcol, code, code4, dupcode = (small[:, 308 + ET * k:320 + ET * k] for k in range(5))

        ps = ctx.enter_context(nc.psum_tensor("ps", [P, 8, 512], f32))
        ACC = ((0, 1), (2, 3))
        TURN = (4, 5)
        EDGE = (6, 7)
        CX = (2, 3, 6, 7)
        PROBS_T = (0, 1, 4, 5)

        def quad(bank, count=4):
            return ps[:, bank, 0:count * N].rearrange("p (c n) -> p c n", n=N)

        x_loaded, xt_loaded, par_loaded = sem("x_loaded"), sem("xt_loaded"), sem("par_loaded")
        erow_loaded, ecol_loaded, rows_loaded = sem("erow_loaded"), sem("ecol_loaded"), sem("rows_loaded")
        loads, users = [], {}
        for n, count, cols, at in transfers():
            key = (cols if n < WIN or n >= WOUT else n < CONV, at)
            if key not in users:
                users[key] = [sem(f"loaded_{n}"), 0]
            users[key][1] += 16
            loads.append((n, count, cols, at, *users[key]))
        stored = [sem(f"stored{h}") for h in range(2)]
        high_ready, low_ready = sem("high_ready"), sem("low_ready")
        used = sem("used")
        consts_ready, keyw_ready = sem("consts_ready"), sem("keyw_ready")
        xh_ready, xl_ready = sem("xh_ready"), sem("xl_ready")
        erow_ready, keys_spread = sem("erow_ready"), sem("keys_spread")
        ecol_ready = sem("ecol_ready")
        later_ready, onehot_ready = sem("later_ready"), sem("onehot_ready")
        dups_done, dup_ready, dw_ready = sem("dups_done"), sem("dup_ready"), sem("dw_ready")
        codes_done, codes_copied, mask_ready = sem("codes_done"), sem("codes_copied"), sem("mask_ready")
        adj_done, adj_copied, cnt_done, adj_ready = sem("adj_done"), sem("adj_copied"), sem("cnt_done"), sem("adj_ready")
        ct_ready = sem("ct_ready")
        w4_abs, w4_exp, w4_log, w4_ready = sem("w4_abs"), sem("w4_exp"), sem("w4_log"), sem("w4_ready")
        flat_ready = sem("flat_ready")
        turned = sem("turned")
        turned_ready = sem("turned_ready")
        hh_ready, hl_ready = sem("hh_ready"), sem("hl_ready")
        scored, masked, maxed = sem("scored"), sem("masked"), sem("maxed")
        shifted, expd, recips, probs_ready = sem("shifted"), sem("expd"), sem("recips"), sem("probs_ready")
        probs_turned, prT_even, prT_odd = sem("probs_turned"), sem("prT_even"), sem("prT_odd")
        v2_done, v2_ready = sem("v2_done"), sem("v2_ready")
        mixed, mixed_ready = sem("mixed"), sem("mixed_ready")
        oh_ready, ol_ready = sem("oh_ready"), sem("ol_ready")
        attended, row_spread, row_copied = sem("attended"), sem("row_spread"), sem("row_copied")
        var_ready, std_ready = sem("var_ready"), sem("std_ready")
        x1_ready, x1_turned, x1h_ready, x1l_ready = sem("x1_ready"), sem("x1_turned"), sem("x1h_ready"), sem("x1l_ready")
        x1b_ready = sem("x1b_ready")
        rows_done = sem("rows_done")
        rows_even, rows_odd = sem("rows_even"), sem("rows_odd")
        back = sem("back")
        relu_ready = sem("relu_ready")
        hx_ready, hxh_ready, hxl_ready = sem("hx_ready"), sem("hxh_ready"), sem("hxl_ready")
        xn_turned, xn_even, xn_odd = sem("xn_turned"), sem("xn_even"), sem("xn_odd")
        cx_done, cxh_ready, cxl_ready = sem("cx_done"), sem("cxh_ready"), sem("cxl_ready")
        out_done, y_ready = sem("out_done"), sem("y_ready")
        dve_step, pool_step = sem("dve_step"), sem("pool_step")

        def source(n, count):
            if n < WIN:
                return wp[P * n:P * (n + count), :]
            if n < CONV:
                return w_in[P * (n - WIN):P * (n - WIN + count), :]
            if n < WOUT:
                return wc[P * (n - CONV):P * (n - CONV + count), :]
            return w_out[P * (n - WOUT):P * (n - WOUT + count), :]

        def raw(n):
            first, _, cols, at, loaded, value = next(t for t in loads if t[0] <= n < t[0] + t[1])
            return ring[:, at + (n - first) * cols:at + (n - first + 1) * cols], loaded, value

        def part(tensor, n):
            cols = F if n < WIN or n >= WOUT else D
            return tensor[:, F * (n % HALVES):F * (n % HALVES) + cols]

        block = ctx.enter_context(nc.Block())

        @block.sync
        def _(sp):
            owner = [0] * RING
            for n, count, cols, at, loaded, _ in loads:
                free = max(owner[at:at + count * cols])
                if free:
                    sp.wait_ge(low_ready, free)
                sp.dma_start(ring[:, at:at + count * cols].rearrange("p (k n) -> p k n", n=cols),
                             source(n, count).rearrange("(k p) n -> p k n", p=P)).then_inc(loaded, 16)
                owner[at:at + count * cols] = [n + count] * (count * cols)
            for h in range(2):
                sp.wait_ge(y_ready, h + 1)
                sp.dma_start(out[:, 512 * h:512 * (h + 1)], y_out[:, 512 * h:512 * (h + 1)]).then_inc(stored[h], 16)
            for h in range(2):
                sp.wait_ge(stored[h], 16)

        @block.gpsimd
        def _(pool):
            steps = [0]

            def step(ins):
                steps[0] += 1
                ins.then_inc(pool_step, 1)
                pool.wait_ge(pool_step, steps[0])

            step(pool.memset(ident[:, :], 0.0))
            pool.affine_select(out=ident[:, :], in_=ident[:, :], compare_op=ALU.not_equal, fill=1.0, base=0,
                               pattern=[[-1, P]], channel_multiplier=1).then_inc(consts_ready, 1)
            pool.memset(ones[:, :], 1.0).then_inc(consts_ready, 1)
            pool.memset(ones_bf, 1.0).then_inc(consts_ready, 1)
            step(pool.memset(keyw, 1.0))
            pool.memset(keyw[0:1, :], float(N)).then_inc(keyw_ready, 1)
            step(pool.memset(tri, 1.0))
            pool.affine_select(out=tri, in_=tri, compare_op=ALU.is_gt, fill=0.0, base=0,
                               pattern=[[-1, P]], channel_multiplier=1).then_inc(consts_ready, 1)
            iota_i = work[:, 6368:6944].bitcast(i32)
            step(pool.iota(iota_i, [[1, R * N]], base=0, channel_multiplier=0))
            pool.tensor_copy(iota, iota_i).then_inc(consts_ready, 1)
            pool.wait_ge(onehot_ready, 3 * ET)
            pool.wait_ge(dup_ready, 1)
            pool.tensor_tensor(Dw, Dh, dupcode.unsqueeze(2).to_broadcast([P, ET, N]), ALU.mult).then_inc(dw_ready, 1)
            pool.wait_ge(codes_copied, 1)
            pool.wait_ge(w4_ready, 1)
            step(pool.tensor_scalar(mtmp, mcode, 0.0, 4.0, ALU.is_equal, ALU.mult))
            step(pool.tensor_tensor(mtmp, mtmp, ident[0:N, 0:N], ALU.mult))
            step(pool.tensor_tensor(mcode, mcode, mtmp, ALU.add))
            step(pool.tensor_scalar(mask, mcode, 0.0, NEG, ALU.is_equal, ALU.mult))
            for k in range(4):
                step(pool.tensor_scalar(mtmp, mcode, float(k + 1), w4[0:N, k:k + 1], ALU.is_equal, ALU.mult))
                last = pool.tensor_tensor(mask, mask, mtmp, ALU.add)
                if k < 3:
                    step(last)
            last.then_inc(mask_ready, 1)
            pool.wait_ge(adj_ready, 1)
            pool.wait_ge(par_loaded, 16)
            term_v = term.rearrange("p (b n) -> p b n", n=N)
            for l in range(L):
                c_l = ct[:, l * B * N:(l + 1) * B * N].rearrange("p (b n) -> p b n", n=N)
                for r in range(R):
                    comp = par[0:N, C_COMP + (l * R + r) * B:C_COMP + (l * R + r + 1) * B]
                    last = pool.tensor_tensor(term_v if r else c_l,
                                              adj[:, N * r:N * (r + 1)].unsqueeze(1).to_broadcast([N, B, N]),
                                              comp.unsqueeze(2).to_broadcast([N, B, N]), ALU.mult)
                    step(last)
                    if r:
                        last = pool.tensor_tensor(c_l, c_l, term_v, ALU.add)
                        if r < R - 1:
                            step(last)
                last.then_inc(ct_ready, 1)
            def scale(k):
                pool.wait_ge(recips, k + 1)
                pool.tensor_tensor(pr[:, k], pr[:, k], rs[0:N, k].unsqueeze(2).to_broadcast([N, 4, N]),
                                   ALU.mult).then_inc(probs_ready, 1)

            for k in range(4):
                pool.wait_ge(maxed, k + 1)
                pool.tensor_tensor(pr[:, k], pr[:, k], mx[0:N, k].unsqueeze(2).to_broadcast([N, 4, N]),
                                   ALU.subtract).then_inc(shifted, 1)
                if k > 1:
                    scale(k - 2)
            scale(2)
            scale(3)
            pool.wait_ge(row_copied, 4)
            pool.wait_ge(x1_ready, 2)
            pool.tensor_tensor(x1b, x1b, x_nat[0:N, :], ALU.add).then_inc(x1b_ready, 1)

        @block.scalar
        def _(act):
            act.dma_start(erow_i, edges).then_inc(erow_loaded, 16)
            act.dma_start(ecol_i, ecols).then_inc(ecol_loaded, 16)
            act.dma_start(turnT[:, :], xt).then_inc(xt_loaded, 16)
            act.dma_start(par[:, :], params).then_inc(par_loaded, 16)
            act.dma_start(x_nat[0:N, :], x).then_inc(x_loaded, 16)
            for k in range(4):
                act.dma_start(rows_sb[32 * k:32 * k + 1, :], rows[k:k + 1, :]).then_inc(rows_loaded, 16)

            def split(n):
                view, loaded, value = raw(n)
                act.wait_ge(loaded, value)
                if n >= HALVES:
                    act.wait_ge(used, n - HALVES + 1)
                act.activation(part(w_high, n), view, ACT.Copy).then_inc(high_ready, 1)

            def copy(dst, src, signal):
                act.activation(dst, src, ACT.Copy).then_inc(signal, 1)

            act.wait_ge(xt_loaded, 16)
            copy(x_high[:, :], turnT[:, :], xh_ready)
            act.wait_ge(w4_abs, 1)
            act.activation(w4e, w4n, ACT.Exp).then_inc(w4_exp, 1)
            act.wait_ge(w4_exp, 1)
            act.activation(w4l, w4e, ACT.Ln, bias=1.0).then_inc(w4_log, 1)
            def rows_of(m):
                act.wait_ge(used, FB * (m + 1))
                if m >= 1:
                    act.wait_ge(turned, m)
                for h in range(2):
                    copy(flat_sb[0:N, 512 * h:512 * (h + 1)], ps[0:N, ACC[m % 2][h], :], flat_ready)

            def high_of(m):
                act.wait_ge(turned_ready, 2 * (m + 1))
                copy(hh[:, SLOT[m]], turned_v, hh_ready)

            for n in range(WO):
                split(n)
                m, i = divmod(n - BEHIND, FB)
                if m >= 1 and i == 0:
                    rows_of(m - 1)
                if m - 1 in SLOT and i == (0 if m == V2 else 2):
                    high_of(m - 1)
                if m == V2 and 2 <= i < 6:
                    act.wait_ge(shifted, i - 1)
                    act.activation(pr[:, i - 2], pr[:, i - 2], ACT.Exp).then_inc(expd, 1)
            for n in range(WO, WO + HALVES):
                split(n)
            act.wait_ge(used, WO)
            copy(v2[:, 0:512], ps[0:N, ACC[V2 % 2][0], :], v2_ready)
            for k in (0, 2):
                act.wait_ge(probs_turned, k // 2 + 1)
                copy(prT[:, k], quad(PROBS_T[k])[0:N], prT_even)
            for h in range(2):
                act.wait_ge(mixed_ready, h + 1)
                copy(hh[:, 0, 4 * h:4 * h + 4, :], turned_v[:, 4 * h:4 * h + 4, :], oh_ready)
            act.activation(dummy, ident[:, 0:1], ACT.Sqrt)
            for n in range(WO + HALVES, WIN + 2):
                split(n)

            def spread(k):
                for h in range(2):
                    act.wait_ge(row_spread, 2 * k + h + 1)
                    copy((gamma_b, x1b)[k][:, 512 * h:512 * (h + 1)], ps[0:N, (TURN, ACC[1])[k][h], :], row_copied)

            def sqrt(v, parts, count):
                act.wait_ge(var_ready, v)
                act.activation(std[0:parts, 0:count], mv[0:parts, 0:count, 1], ACT.Sqrt,
                               bias=eps[0:parts, :]).then_inc(std_ready, 1)

            spread(0)
            sqrt(1, N, 1)
            spread(1)
            split(WIN + 2)
            for h in range(2):
                act.wait_ge(x1_turned, h + 1)
                copy(xh[:, 4 * h:4 * h + 4, :], quad(EDGE[h]), x1h_ready)
            for n in range(WIN + 3, CONV + 2):
                split(n)

            def from_rows(c):
                act.wait_ge(rows_done, c + 1)
                copy(flat_sb[0:N, 0:384], ps[0:N, ACC[0][0], 0:384], rows_even)
                to, bias = (rT, C_CONV + (c - 1) * DB) if c else (hx, C_BIN)
                for o in range(DB):
                    if o % 3 == 0:
                        act.wait_ge(back, 2 * c + o // 3 + 1)
                    act.activation(to[:, o, :], quad(TURN[o // 3])[:, o % 3], ACT.Relu,
                                   bias=par[:, bias + o:bias + o + 1]).then_inc(relu_ready, 1)

            from_rows(0)
            for h in range(2):
                act.wait_ge(relu_ready, 3 * (h + 1))
                copy(xh[:, 3 * h:3 * h + 3, :], hx[:, 3 * h:3 * h + 3, :], hxh_ready)
            split(CONV + 2)
            for l in range(L):
                base = CONV + l * LAYER
                act.wait_ge(xn_turned, 2 * l + 1)
                copy(xn[:, 0:512], ps[0:N, EDGE[0], :], xn_even)
                for k in range(HALVES, LAYER + 2):
                    split(base + k)
                    if k == DB + 2:
                        for i in range(DB):
                            act.wait_ge(cx_done, DB * l + i + 1)
                            copy(cxh[:, i], quad(CX[i % 4]), cxh_ready)
                from_rows(l + 1)
                sqrt(l + 2, P, DB)
                for h in range(2):
                    act.wait_ge(hx_ready, DB * l + 3 * (h + 1))
                    copy(xh[:, 3 * h:3 * h + 3, :], hx[:, 3 * h:3 * h + 3, :], hxh_ready)
                split(base + LAYER + 2)
            for n in range(WOUT + HALVES, BLOCKS):
                split(n)
            sqrt(L + 2, N, 1)
            sqrt(L + 3, N, 1)

        @block.vector
        def _(dve):
            steps = [0]

            def step(ins):
                steps[0] += 1
                ins.then_inc(dve_step, 1)
                dve.wait_ge(dve_step, steps[0])

            def split(n):
                view, _, _ = raw(n)
                dve.wait_ge(high_ready, n + 1)
                dve.tensor_tensor(part(w_low, n), view, part(w_high, n).bitcast(f32),
                                  ALU.subtract).then_inc(low_ready, 1)

            step(dve.memset(eps, EPS))
            dve.wait_ge(erow_loaded, 16)
            dve.tensor_copy(erow, erow_i).then_inc(erow_ready, 1)
            dve.wait_ge(ecol_loaded, 16)
            step(dve.tensor_copy(ecol, ecol_i))
            step(dve.tensor_scalar(code4, typ5, 0.0, 4.0, ALU.is_equal, ALU.mult))
            step(dve.tensor_tensor(code, code4, typ5, ALU.add))
            for t in range(1, ET):
                dve.tensor_scalar(code[:, t:t + 1], code[:, t:t + 1], float(16 ** t), None, ALU.mult)
            dve.scalar_tensor_tensor(relcol, typ6, float(N), dst, ALU.mult, ALU.add)
            step(dve.scalar_tensor_tensor(keycol, src, float(N), dst, ALU.mult, ALU.add))
            dve.wait_ge(xh_ready, 1)
            dve.tensor_tensor(x_low[:, :], turnT[:, :], x_high[:, :].bitcast(f32), ALU.subtract).then_inc(xl_ready, 1)
            dve.wait_ge(par_loaded, 16)
            etw = par[:, C_ETW:C_ETW + 4]
            step(dve.tensor_scalar(w4n, etw, -1.0, None, ALU.mult))
            dve.tensor_tensor(w4n, w4n, etw, ALU.min).then_inc(w4_abs, 1)
            dve.wait_ge(keys_spread, 1)
            dve.wait_ge(consts_ready, 5)
            for t in range(ET):
                last = dve.scalar_tensor_tensor(later[:, t, :], ps[:, 4 + t // 4, P * (t % 4):P * (t % 4 + 1)],
                                                keycol[:, t:t + 1], tri, ALU.is_equal, ALU.mult)
            last.then_inc(later_ready, 1)
            dve.wait_ge(w4_log, 1)
            dve.scalar_tensor_tensor(w4, etw, 0.0, w4l, ALU.max, ALU.add).then_inc(w4_ready, 1)

            def mask_scores(k):
                dve.wait_ge(scored, k + 1)
                step(dve.scalar_tensor_tensor(pr[:, k], quad(4 + k)[0:N], SCALE,
                                              mask.unsqueeze(1).to_broadcast([N, 4, N]), ALU.mult, ALU.add))
                dve.tensor_reduce(mx[0:N, k], pr[:, k], AX.X, ALU.max).then_inc(maxed, 1)

            def total(k):
                dve.wait_ge(expd, k + 1)
                step(dve.tensor_reduce(sm[0:N, k], pr[:, k], AX.X, ALU.add))
                dve.reciprocal(rs[0:N, k], sm[0:N, k]).then_inc(recips, 1)

            def bias_of(m, banks):
                to = {Q2: q2T, K2: k2T}.get(m, turned_v)
                dve.wait_ge(turned, m + 1)
                for h in range(2):
                    bias = par[:, FB * m + 4 * h:FB * m + 4 * h + 4]
                    dve.tensor_tensor(to[:, 4 * h:4 * h + 4, :], quad(banks[h]),
                                      bias.unsqueeze(2).to_broadcast([P, 4, N]), ALU.add).then_inc(turned_ready, 1)
                if m in SLOT:
                    dve.wait_ge(hh_ready, SLOT[m] + 1)
                    dve.tensor_tensor(hl[:, SLOT[m]], turned_v, hh[:, SLOT[m]].bitcast(f32),
                                      ALU.subtract).then_inc(hl_ready, 1)

            for n in range(WO):
                split(n)
                if n < ET:
                    for hot, count, col in ((S, N, src), (Dh, N, dst), (D6, R * N, relcol)):
                        dve.tensor_scalar(hot[:, n, :], iota[:, 0:count], col[:, n:n + 1], None,
                                          ALU.is_equal).then_inc(onehot_ready, 1)
                if n == DUPS_AT + BEHIND:
                    dve.wait_ge(dups_done, 1)
                    dve.scalar_tensor_tensor(dupcode, ps[:, EDGE[1], 0:ET], 0.0, code, ALU.is_equal,
                                             ALU.mult).then_inc(dup_ready, 1)
                if n == ADJ_AT + BEHIND:
                    for h in range(2):
                        dve.wait_ge(adj_done, h + 1)
                        dve.tensor_copy(adj[:, 288 * h:288 * (h + 1)], ps[0:N, EDGE[h], 0:288]).then_inc(adj_copied, 1)
                if n == CNT_AT + BEHIND:
                    for h in range(2):
                        dve.wait_ge(cnt_done, h + 1)
                        step(dve.tensor_scalar(cnt[:, 288 * h:288 * (h + 1)], ps[0:N, EDGE[h], 0:288], 1.0, None,
                                               ALU.max))
                    step(dve.reciprocal(cnt, cnt))
                    dve.wait_ge(adj_copied, 2)
                    dve.tensor_tensor(adj, adj, cnt, ALU.mult).then_inc(adj_ready, 1)
                if n == CODES_AT + BEHIND:
                    dve.wait_ge(codes_done, 1)
                    step(dve.tensor_copy(msum, ps[0:N, EDGE[0], 0:N]))
                    step(dve.tensor_scalar(mbits.bitcast(i32), msum.bitcast(i32), 22, 7,
                                           ALU.logical_shift_right, ALU.bitwise_and))
                    step(dve.tensor_copy(mlead, mbits.bitcast(i32)))
                    step(dve.tensor_scalar(mtmp, mlead, 6.0, -7.0, ALU.is_equal, ALU.mult))
                    step(dve.scalar_tensor_tensor(mtmp, mlead, 2.0, mtmp, ALU.add, ALU.add))
                    dve.scalar_tensor_tensor(mcode, msum, 0.0, mtmp, ALU.is_gt, ALU.mult).then_inc(codes_copied, 1)
                m, i = divmod(n - BEHIND, FB)
                if m >= 1 and m != V2 and i == 2:
                    bias_of(m - 1, TURN)
                if m == V2 and i == 0:
                    bias_of(V1, ACC[0])
                    dve.wait_ge(mask_ready, 1)
                if m == V2 and i < 4:
                    mask_scores(i)
                if m == V2 and i >= 3:
                    total(i - 3)
            split(WO)
            total(3)
            split(WO + 1)
            split(WO + 2)
            dve.wait_ge(used, WO)
            dve.tensor_copy(v2[:, 512:1024], ps[0:N, ACC[V2 % 2][1], :]).then_inc(v2_ready, 1)
            for k in (1, 3):
                dve.wait_ge(probs_turned, k // 2 + 1)
                dve.tensor_copy(prT[:, k], quad(PROBS_T[k])[0:N]).then_inc(prT_odd, 1)
            for h in range(2):
                bias = par[:, FB * V2 + 4 * h:FB * V2 + 4 * h + 4]
                dve.wait_ge(mixed, h + 1)
                dve.tensor_tensor(turned_v[:, 4 * h:4 * h + 4, :], quad(EDGE[h]),
                                  bias.unsqueeze(2).to_broadcast([P, 4, N]), ALU.add).then_inc(mixed_ready, 1)
            for h in range(2):
                dve.wait_ge(oh_ready, h + 1)
                dve.tensor_tensor(hl[:, 0, 4 * h:4 * h + 4, :], turned_v[:, 4 * h:4 * h + 4, :],
                                  hh[:, 0, 4 * h:4 * h + 4, :].bitcast(f32), ALU.subtract).then_inc(ol_ready, 1)
            for n in range(WO + HALVES, WIN + 2):
                split(n)

            def half_stats(h, view):
                step(dve.bn_stats(st[0:N, h, :], view))

            def half_std(v):
                dve.bn_aggr(mv[0:N, 0, :], st[0:N, 0:2, :]).then_inc(var_ready, 1)

            def half_rstd(v):
                dve.wait_ge(std_ready, v)
                step(dve.reciprocal(rstd[0:N, 0:1], std[0:N, 0:1]))

            def normalize(to, view, signal):
                dve.tensor_scalar(to, view, mv[0:N, 0, 0:1], rstd[0:N, 0:1],
                                  ALU.subtract, ALU.mult).then_inc(signal, 1)

            dve.wait_ge(x_loaded, 16)
            for h in range(2):
                half = slice(512 * h, 512 * (h + 1))
                dve.wait_ge(*((attended, 1), (used, WIN))[h])
                step(dve.tensor_tensor(r1[:, half], ps[0:N, ACC[0][h], :], x_nat[0:N, half], ALU.add))
                half_stats(h, r1[:, half])
            half_std(1)
            half_rstd(1)
            for h in range(2):
                half = slice(512 * h, 512 * (h + 1))
                normalize(x_nat[0:N, half], r1[:, half], x1_ready)
            split(WIN + 2)
            for h in range(2):
                dve.wait_ge(x1h_ready, h + 1)
                dve.tensor_tensor(xl[:, 4 * h:4 * h + 4, :], quad(EDGE[h]), xh[:, 4 * h:4 * h + 4, :].bitcast(f32),
                                  ALU.subtract).then_inc(x1l_ready, 1)
            for n in range(WIN + 3, CONV + 2):
                split(n)

            def rest_of_rows(c):
                dve.wait_ge(used, CONV + c * LAYER)
                dve.tensor_copy(flat_sb[0:N, 384:768], ps[0:N, ACC[0][1], 0:384]).then_inc(rows_odd, 1)

            def low_of_hx(c):
                for h in range(2):
                    dve.wait_ge(hxh_ready, 2 * c + h + 1)
                    dve.tensor_tensor(xl[:, 3 * h:3 * h + 3, :], hx[:, 3 * h:3 * h + 3, :],
                                      xh[:, 3 * h:3 * h + 3, :].bitcast(f32), ALU.subtract).then_inc(hxl_ready, 1)

            rest_of_rows(0)
            low_of_hx(0)
            split(CONV + 2)
            for l in range(L):
                base = CONV + l * LAYER
                dve.wait_ge(xn_turned, 2 * l + 2)
                dve.tensor_copy(xn[:, 512:768], ps[0:N, EDGE[1], 0:256]).then_inc(xn_odd, 1)
                for k in range(HALVES, LAYER + 2):
                    split(base + k)
                    if k == DB + 2:
                        for i in range(DB):
                            dve.wait_ge(cxh_ready, DB * l + i + 1)
                            dve.tensor_tensor(cxl[:, i], quad(CX[i % 4]), cxh[:, i].bitcast(f32),
                                              ALU.subtract).then_inc(cxl_ready, 1)
                rest_of_rows(l + 1)
                for h in range(2):
                    third = slice(3 * h, 3 * h + 3)
                    dve.wait_ge(relu_ready, (l + 1) * DB + 3 * (h + 1))
                    step(dve.tensor_tensor(rT[:, third, :], rT[:, third, :], hx[:, third, :], ALU.add))
                    for o in range(3 * h, 3 * h + 3):
                        last = dve.bn_stats(st[:, o, :], rT[:, o, :])
                step(last)
                for o in range(DB):
                    last = dve.bn_aggr(mv[:, o, :], st[:, o, :])
                last.then_inc(var_ready, 1)
                dve.wait_ge(std_ready, l + 2)
                step(dve.reciprocal(rstd, std))
                gamma = par[:, C_GAMMA + l * DB:C_GAMMA + (l + 1) * DB]
                beta = par[:, C_BETA + l * DB:C_BETA + (l + 1) * DB]
                step(dve.tensor_tensor(bn_a, rstd, gamma, ALU.mult))
                step(dve.tensor_tensor(bn_m, mv[:, 0:DB, 0], bn_a, ALU.mult))
                step(dve.tensor_tensor(bn_c, beta, bn_m, ALU.subtract))
                for o in range(DB):
                    dve.tensor_scalar(hx[:, o, :], rT[:, o, :], bn_a[:, o:o + 1], bn_c[:, o:o + 1],
                                      ALU.mult, ALU.add).then_inc(hx_ready, 1)
                low_of_hx(l + 1)
                split(base + LAYER + 2)
            for n in range(WOUT + HALVES, BLOCKS):
                split(n)
            for h in range(2):
                dve.wait_ge(*((out_done, 1), (used, BLOCKS))[h])
                half_stats(h, ps[0:N, ACC[0][h], :])
            half_std(L + 2)
            dve.wait_ge(x1b_ready, 1)
            half_rstd(L + 2)
            for h in range(2):
                half = slice(512 * h, 512 * (h + 1))
                step(dve.scalar_tensor_tensor(h2[:, half], ps[0:N, ACC[0][h], :], mv[0:N, 0, 0:1], gamma_b[:, half],
                                              ALU.subtract, ALU.mult))
                step(dve.scalar_tensor_tensor(h2[:, half], h2[:, half], rstd[0:N, 0:1], x1b[:, half],
                                              ALU.mult, ALU.add))
                half_stats(h, h2[:, half])
            half_std(L + 3)
            half_rstd(L + 3)
            for h in range(2):
                half = slice(512 * h, 512 * (h + 1))
                normalize(y_out[:, half], h2[:, half], y_ready)

        @block.tensor
        def _(pe):
            pe.wait_ge(consts_ready, 5)
            pe.wait_ge(erow_ready, 1)
            pe.wait_ge(keyw_ready, 1)
            for c in range(3):
                last = pe.matmul(ps[:, 4 + c, :], keyw, erow[:, 512 * c:512 * (c + 1)], start=True, stop=True)
            last.then_inc(keys_spread, 1)

            def product(n, buf, high, low, first, end, at=0, done=None):
                cols = F if n < WIN or n >= WOUT else D
                w = cols // 2
                pe.wait_ge(high_ready, at + (n + 1))
                for weight, left in ((w_high, high), (w_high, low), (w_low, high)):
                    if weight is w_low:
                        pe.wait_ge(low_ready, at + (n + 1))
                    for h in range(2):
                        last = pe.matmul(ps[0:N, buf[h], 0:w], left, part(weight, n)[:, w * h:w * (h + 1)],
                                         start=first and weight is w_high and left is high, stop=end and weight is w_low,
                                         skip_group_check=True)
                        if done is not None and weight is w_low and h == 0:
                            last.then_inc(done, 1)
                last.then_inc(used, 1)

            def turn(m, banks):
                pe.wait_ge(flat_ready, 2 * (m + 1))
                if 1 <= m < V1:
                    pe.wait_ge(turned_ready, 2 * m)
                for i in range(FB):
                    last = pe.transpose(quad(banks[i // 4])[:, i % 4], flat_sb[0:N, P * i:P * (i + 1)],
                                        ident[0:N, 0:N])
                last.then_inc(turned, 1)

            for n in range(WO):
                m, i = divmod(n, FB)
                if n == 0:
                    pe.wait_ge(xl_ready, 1)
                if n == FB * V2:
                    pe.wait_ge(turned_ready, 2 * (K2 + 1))
                    pe.wait_ge(codes_copied, 1)
                    for half in range(2):
                        for c in range(4):
                            for odd in range(2):
                                hd = slice(HD * odd, HD * (odd + 1))
                                last = pe.matmul(quad(4 + 2 * half + odd)[0:N, c], q2T[hd, 4 * half + c, :],
                                                 k2T[hd, 4 * half + c, :], start=True, stop=True)
                                if c == 3:
                                    last.then_inc(scored, 1)
                    turn(V1, ACC[0])
                if i == 0 and m in (Q2, K2, V2):
                    pe.wait_ge(hl_ready, {Q2: 1, K2: 2, V2: 3}[m])
                slot = {Q2: 0, K2: 1, V2: 2}.get(m)
                high, low = (xh, xl) if slot is None else (hh[:, slot], hl[:, slot])
                product(n, ACC[m % 2], high[:, i, :], low[:, i, :], i == 0, i == FB - 1)
                if 1 <= m < V2 and i == 1:
                    if m == 1:
                        pe.wait_ge(later_ready, 1)
                    turn(m - 1, TURN)
                if n == DUPS_AT:
                    pe.wait_ge(later_ready, 1)
                    for t in range(ET):
                        last = pe.matmul(ps[:, EDGE[1], t:t + 1], later[:, t, :], ones_bf, start=True, stop=True)
                    last.then_inc(dups_done, 1)
                if n == ADJ_AT:
                    pe.wait_ge(onehot_ready, 3 * ET)
                    pe.wait_ge(dup_ready, 1)
                    for h in range(2):
                        for t in range(ET):
                            last = pe.matmul(ps[0:N, EDGE[h], 0:288], S[:, t, :], D6[:, t, 288 * h:288 * (h + 1)],
                                             start=(t == 0), stop=(t == ET - 1))
                        last.then_inc(adj_done, 1)
                if n == CNT_AT:
                    pe.wait_ge(adj_copied, 2)
                    for h in range(2):
                        pe.matmul(ps[0:N, EDGE[h], 0:288], ones[0:N, :], adj[:, 288 * h:288 * (h + 1)],
                                  start=True, stop=True).then_inc(cnt_done, 1)
                if n == CODES_AT:
                    pe.wait_ge(adj_ready, 1)
                    pe.wait_ge(dw_ready, 1)
                    for t in range(ET):
                        last = pe.matmul(ps[0:N, EDGE[0], 0:N], S[:, t, :], Dw[:, t, :],
                                         start=(t == 0), stop=(t == ET - 1))
                    last.then_inc(codes_done, 1)
            for h in range(2):
                pe.wait_ge(probs_ready, 2 * h + 2)
                for k in (2 * h, 2 * h + 1):
                    for c in range(4):
                        last = pe.transpose(quad(PROBS_T[k])[0:N, c], pr[:, k, c], ident[0:N, 0:N])
                last.then_inc(probs_turned, 1)
            pe.wait_ge(v2_ready, 2)
            for h in range(2):
                pe.wait_ge(prT_even, h + 1)
                pe.wait_ge(prT_odd, h + 1)
                for c in range(4):
                    for odd in range(2):
                        head = 8 * h + 2 * c + odd
                        last = pe.matmul(quad(EDGE[h])[HD * odd:HD * (odd + 1), c], v2[:, HD * head:HD * (head + 1)],
                                         prT[:, 2 * h + odd, c], start=True, stop=True)
                last.then_inc(mixed, 1)

            def spread(row, h, bank, stop):
                return pe.matmul(ps[0:N, bank, :], ones[32 * row:32 * row + 1, :],
                                 rows_sb[32 * row:32 * row + 1, 512 * h:512 * (h + 1)],
                                 start=True, stop=stop, skip_group_check=True)

            pe.wait_ge(rows_loaded, 64)
            for h in range(2):
                spread(0, h, ACC[0][h], False)
            for i in range(FB):
                if i % 4 == 0:
                    pe.wait_ge(ol_ready, i // 4 + 1)
                product(WO + i, ACC[0], hh[:, 0, i, :], hl[:, 0, i, :], False, i == FB - 1,
                        done=attended if i == FB - 1 else None)
            for k in range(2):
                for h in range(2):
                    spread(2 + k, h, (TURN, ACC[1])[k][h], True).then_inc(row_spread, 1)
            for i in range(FB):
                if i % 4 == 0:
                    pe.wait_ge(x1_ready, i // 4 + 1)
                last = pe.transpose(quad(EDGE[i // 4])[:, i % 4], x_nat[0:N, P * i:P * (i + 1)], ident[0:N, 0:N])
                if i % 4 == 3:
                    last.then_inc(x1_turned, 1)
            for i in range(FB):
                if i % 4 == 0:
                    pe.wait_ge(x1l_ready, i // 4 + 1)
                product(WIN + i, ACC[0], xh[:, i, :], xl[:, i, :], i == 0, i == FB - 1,
                        done=rows_done if i == FB - 1 else None)
            pe.wait_ge(row_copied, 4)

            def back_from_rows(c):
                for o in range(DB):
                    if o % 3 == 0:
                        pe.wait_ge((rows_even, rows_odd)[o // 3], c + 1)
                    last = pe.transpose(quad(TURN[o // 3])[:, o % 3], flat_sb[0:N, P * o:P * (o + 1)],
                                        ident[0:N, 0:N])
                    if o % 3 == 2:
                        last.then_inc(back, 1)

            back_from_rows(0)
            with pe.Fori(0, L) as l:
                for o in range(DB):
                    if o % 3 == 0:
                        pe.wait_ge(hxl_ready, 2 * l + (o // 3 + 1))
                    last = pe.transpose(ps[0:N, EDGE[o // 4], P * (o % 4):P * (o % 4 + 1)], hx[:, o, :], ident[:, :])
                    if o in (3, DB - 1):
                        last.then_inc(xn_turned, 1)
                for i in range(DB):
                    product(CONV + i, ACC[0], xh[:, i, :], xl[:, i, :], i == 0, False, at=l * LAYER)
                pe.wait_ge(xn_even, l + 1)
                pe.wait_ge(xn_odd, l + 1)
                pe.wait_ge(ct_ready, l + 1)
                for i in range(DB):
                    if i >= 4:
                        pe.wait_ge(cxl_ready, l * DB + (i - 3))
                    pe.matmul(ps[:, CX[i % 4], 0:B * N], xn[:, P * i:P * (i + 1)],
                              ct[:, ds(l * (B * N), B * N)], start=True, stop=True).then_inc(cx_done, 1)
                for b in range(B):
                    for i in range(DB):
                        if b == 0:
                            pe.wait_ge(cxl_ready, l * DB + (i + 1))
                        k = DB * (1 + b) + i
                        product(CONV + k, ACC[0], cxh[:, i, b, :], cxl[:, i, b, :], False, k == LAYER - 1,
                                at=l * LAYER, done=rows_done if k == LAYER - 1 else None)
                back_from_rows(l + 1)
            pe.wait_ge(hxl_ready, 2 * (L + 1))
            for h in range(2):
                spread(1, h, ACC[0][h], False)
            for i in range(DB):
                product(WOUT + i, ACC[0], xh[:, i, :], xl[:, i, :], False, i == DB - 1,
                        done=out_done if i == DB - 1 else None)


def kernel(**a):
    import concourse.bacc as bacc
    from concourse.bass_utils import run_bass_kernel_spmd

    def cols(*vectors):
        return np.concatenate([v.reshape(-1, P).T for v in vectors], axis=1)

    def spread(v):
        return np.broadcast_to(v.reshape(1, -1), (P, v.size))

    a = {name: np.asarray(v) for name, v in a.items()}
    g0, g1 = "L0_gnn_", "L1_gnn_"
    edges = np.stack([a[n] for n in ("src", "dst", "edge_type_5", "edge_type_6")])
    arrays = {
        "x": a["x"],
        "xt": np.ascontiguousarray(a["x"].T.reshape(FB, P, N).transpose(1, 0, 2).reshape(P, FB * N)),
        "edges": edges[0:2],
        "ecols": np.ascontiguousarray(edges.reshape(4 * ET, P).T),
        "params": np.ascontiguousarray(np.concatenate(
            [cols(*[a[g0 + "b" + n] for n in ORDER], a[g1 + "b_in"], a[g1 + "conv_bias"],
                  a[g1 + "bn_gamma"], a[g1 + "bn_beta"]),
             spread(a[g1 + "comp"]), spread(a[g0 + "edge_type_weights"])], axis=1)),
        "rows": np.stack([a[g0 + "bo"], a[g1 + "b_out"], a[g1 + "ln_gamma"], a[g1 + "ln_beta"]]),
        "wp": np.concatenate([a[g0 + "w" + n].T for n in (*ORDER, "o")]),
        "w_in": a[g1 + "w_in"],
        "wc": np.concatenate([a[g1 + "root"][:, None], a[g1 + "basis"]], axis=1).reshape(L * LAYER * P, D),
        "w_out": a[g1 + "w_out"],
    }
    nc = bacc.Bacc("TRN2", target_bir_lowering=False, num_devices=1)
    aps = {n: nc.dram_tensor(f"in_{n}", v.shape, mybir.dt.from_np(v.dtype), kind="ExternalInput").ap()
           for n, v in arrays.items()}
    out = nc.dram_tensor("out", (N, F), mybir.dt.float32, kind="ExternalOutput").ap()
    gnn_kernel(nc, out=out, **aps)
    result = run_bass_kernel_spmd(nc, [{f"in_{n}": v for n, v in arrays.items()}], core_ids=[0])
    return result.results[0]["out"]
```

```python
import numpy as np
import concourse.bass as bass
from concourse import mybir
from contextlib import ExitStack

N = 96
E = 1536
F = 1024
HEADS = 16
HD = F // HEADS
D = 768
R = 6
B = 4
L = 2
P = 128
FB = F // P
DB = D // P
ET = E // P
EPS = 1e-5
SCALE = 1.0 / float(np.sqrt(np.float32(HD)))
NEG = -3.0e38

C_BIAS0 = 0
C_BIN = C_BIAS0 + 6 * FB
C_CONV = C_BIN + DB
C_GAMMA = C_CONV + L * DB
C_BETA = C_GAMMA + L * DB
C_COMP = C_BETA + L * DB
C_ETW = C_COMP + L * R * B
NPAR = C_ETW + 4

ORDER = ("q", "k", "iq", "ik", "v", "iv")
Q1, K1, Q2, K2, V1, V2 = range(6)

PROJ = 0
WO = PROJ + 6 * FB
WIN = WO + FB
CONV = WIN + FB
LAYER = DB * (1 + B)
WOUT = CONV + L * LAYER
BLOCKS = WOUT + DB
SLOT = {Q1: 0, K1: 1, V1: 2}
DUPS_AT, ADJ_AT, CNT_AT, CODES_AT = 8, 17, 21, 25
BEHIND = 3
RING = LAYER * D
AHEAD = 2
WARMERS = {"start": 16, "v2": 14, "wo": 3, "w_in": 6, "layer": 16, "layer end": 10, "w_out": 8}
PARTS = 4 * F


def by_pool(n):
    if n < CONV:
        return n in (3, 6, 8, 10, 12, 14, 16, 20, 25, 28, 30, 35, 40, 42, WO + 1, WO + 2, WIN + 1, WIN + 4)
    return n % 5 == 0 or (n - CONV) % LAYER in (2, 3)


def by_pool_before(n):
    return sum(by_pool(k) for k in range(n))


def buffer(n):
    def place(k):
        if WIN <= k < WOUT:
            return (k - WIN) % 5 * D, D
        return (k % 4 if k < WIN else (k - WOUT + 3) % 4) * F, F
    at, cols = place(n)
    before = [k + 1 for k in range(n) if place(k)[0] < at + cols and at < sum(place(k))]
    return slice(at, at + cols), max(before, default=0)


def transfers():
    out = [(n, 1, F, n * F) for n in range(2)]
    out += [(n, 2, F, n % (RING // F) * F) for n in range(2, WIN, 2)]
    out += [(WIN + 3 * g, min(3, FB - 3 * g), D, (7 + g) * 3 * D) for g in range(3)]
    out += [(n, 3, D, (n - CONV) % LAYER * D) for n in range(CONV, WOUT, 3)]
    return out + [(n, 2, F, (n - WOUT) * F) for n in range(WOUT, BLOCKS, 2)]


def gnn_kernel(nc, x, xt, edges, ecols, params, rows, wp, w_in, wc, w_out, out):
    f32, f32r, bf16, f16 = mybir.dt.float32, mybir.dt.float32r, mybir.dt.bfloat16, mybir.dt.float16
    i32 = mybir.dt.int32
    ALU, ACT, AX = mybir.AluOpType, mybir.ActivationFunctionType, mybir.AxisListType
    ds = bass.ds

    ctx = ExitStack()
    with ctx:
        def sb(name, cols, dt=f32, parts=P):
            return ctx.enter_context(nc.sbuf_tensor(name, [parts, cols], dt))

        def sem(name):
            return ctx.enter_context(nc.semaphore(name))

        ring = sb("ring", RING)
        w_high = sb("w_high", PARTS, f32r)
        w_low = sb("w_low", PARTS, f32r)
        x_high = sb("x_high", FB * N, f32r)
        x_low = sb("x_low", FB * N, f32r)
        h_high = sb("h_high", DB * B * N, f32r)
        h_low = sb("h_low", DB * B * N, f32r)
        par = sb("par", NPAR)
        rows_sb = sb("rows_sb", F)
        ident = sb("ident", P)
        ones = sb("ones", N)
        x_nat = sb("x_nat", F)
        turnT = sb("turnT", FB * N)
        flat_sb = sb("flat", F)
        work = sb("work", 8960)
        small = sb("small", 512)

        def blocks(view, width=N):
            return view.rearrange("p (k n) -> p k n", n=width)

        xh, xl, turned_v = blocks(x_high[:, :]), blocks(x_low[:, :]), blocks(turnT[:, :])
        cxh = h_high[:, :].rearrange("p (i b n) -> p i b n", b=B, n=N)
        cxl = h_low[:, :].rearrange("p (i b n) -> p i b n", b=B, n=N)
        hh = h_high[:, :].rearrange("p (s k n) -> p s k n", s=3, n=N)
        hl = h_low[:, :].rearrange("p (s k n) -> p s k n", s=3, n=N)
        probs, probsT = work[0:N, 0:1536], work[:, 1536:3072]
        pr = probs.rearrange("p (k c n) -> p k c n", c=4, n=N)
        prT = probsT[0:N, :].rearrange("p (k c n) -> p k c n", c=4, n=N)
        v2 = work[0:N, 3072:4096]
        q2T, k2T = blocks(work[:, 4096:4864]), blocks(work[:, 4864:5632])
        gamma_b, x1b = work[0:N, 4096:5120], work[0:N, 5120:6144]
        ct = work[0:N, 8192:8960]
        r1, y_out = probs[:, 0:F], probs[:, 0:F]
        hx = blocks(probsT[:, 0:DB * N])
        rT = blocks(probsT[:, DB * N:2 * DB * N])
        xn = flat_sb[0:N, 0:D]
        h2 = v2

        erow_i = work[0:2, 0:1536].bitcast(i32)
        erow = work[0:2, 1536:2304].bitcast(bf16)
        D6 = blocks(work[:, 0:3456].bitcast(bf16), R * N)
        S = blocks(work[:, 3456:4032].bitcast(bf16))
        Dh = blocks(work[:, 4032:4608].bitcast(bf16))
        Dw = blocks(work[:, 4608:5184].bitcast(bf16))
        later = blocks(work[:, 5184:5952].bitcast(bf16), P)
        tri = work[:, 5952:6080]
        iota = work[:, 6080:6368].bitcast(f16)
        adj = work[0:N, 6368:6944]
        cnt = work[0:N, 6944:7520]
        term = work[0:N, 7520:7904]
        mcode, mtmp, mbits = (work[0:N, 7904 + N * k:8000 + N * k] for k in range(3))
        msum, mlead = work[0:N, 7520:7616], work[0:N, 7616:7712]
        mask = small[0:N, 400:496]

        st = small[:, 0:36].rearrange("p (k s) -> p k s", s=6)
        mv = small[:, 36:48].rearrange("p (k s) -> p k s", s=2)
        std, rstd = small[:, 48:54], small[:, 54:60]
        bn_a, bn_c, bn_m = small[:, 60:66], small[:, 66:72], small[:, 72:78]
        mx = small[:, 80:96].rearrange("p (k c) -> p k c", c=4)
        sm = small[:, 96:112].rearrange("p (k c) -> p k c", c=4)
        rs = small[:, 112:128].rearrange("p (k c) -> p k c", c=4)
        w4, w4n, w4e, w4l = (small[:, 128 + 4 * k:132 + 4 * k] for k in range(4))
        eps, dummy = small[:, 144:145], small[:, 145:146]
        ones_bf = small[:, 146:147].bitcast(bf16)[:, 0:1]
        keyw = small[0:2, 148:212].bitcast(bf16)
        ecol_i = small[:, 212:260].bitcast(i32)
        ecol = small[:, 260:308]
        src, dst, typ5, typ6 = (ecol[:, ET * k:ET * (k + 1)] for k in range(4))
        keycol, relcol, code, code4, dupcode = (small[:, 308 + ET * k:320 + ET * k] for k in range(5))

        ps = ctx.enter_context(nc.psum_tensor("ps", [P, 8, 512], f32))
        ACC = ((0, 1), (2, 3))
        TURN = (4, 5)
        EDGE = (6, 7)
        CX = (2, 3, 6, 7)
        PROBS_T = (4, 5, 6, 7)

        def quad(bank, count=4):
            return ps[:, bank, 0:count * N].rearrange("p (c n) -> p c n", n=N)

        x_loaded, xt_loaded, par_loaded = sem("x_loaded"), sem("xt_loaded"), sem("par_loaded")
        erow_loaded, ecol_loaded, rows_loaded = sem("erow_loaded"), sem("ecol_loaded"), sem("rows_loaded")
        loads, users = [], {}
        for n, count, cols, at in transfers():
            key = (cols if n < WIN or n >= WOUT else n < CONV, at)
            if key not in users:
                users[key] = [sem(f"loaded_{n}"), 0]
            users[key][1] += 16
            loads.append((n, count, cols, at, *users[key]))
        stored = [sem(f"stored{h}") for h in range(2)]
        high_ready = sem("high_ready")
        low_ready, low_ready_pool = sem("low_ready"), sem("low_ready_pool")
        used = sem("used")
        consts_ready, keyw_ready = sem("consts_ready"), sem("keyw_ready")
        xh_ready, xl_ready = sem("xh_ready"), sem("xl_ready")
        erow_ready, keys_spread = sem("erow_ready"), sem("keys_spread")
        later_ready, onehot_ready = sem("later_ready"), sem("onehot_ready")
        dups_done, dup_ready, dw_ready = sem("dups_done"), sem("dup_ready"), sem("dw_ready")
        codes_done, codes_copied, mask_ready = sem("codes_done"), sem("codes_copied"), sem("mask_ready")
        adj_done, adj_copied, cnt_done = sem("adj_done"), sem("adj_copied"), sem("cnt_done")
        cnt_copied, adj_ready = sem("cnt_copied"), sem("adj_ready")
        ct_ready = sem("ct_ready")
        w4_abs, w4_exp, w4_log, w4_ready = sem("w4_abs"), sem("w4_exp"), sem("w4_log"), sem("w4_ready")
        flat_ready = sem("flat_ready")
        turned = sem("turned")
        turned_ready = sem("turned_ready")
        hh_ready, hl_ready = sem("hh_ready"), sem("hl_ready")
        scored, maxed = sem("scored"), sem("maxed")
        shifted, expd, recips, probs_ready = sem("shifted"), sem("expd"), sem("recips"), sem("probs_ready")
        probs_turned, prT_even, prT_odd = sem("probs_turned"), sem("prT_even"), sem("prT_odd")
        v2_done, v2_even, v2_odd = sem("v2_done"), sem("v2_even"), sem("v2_odd")
        mixed, mixed_ready = sem("mixed"), sem("mixed_ready")
        oh_ready, ol_ready = sem("oh_ready"), sem("ol_ready")
        attended, row_spread, row_copied = sem("attended"), sem("row_spread"), sem("row_copied")
        var_ready, std_ready = sem("var_ready"), sem("std_ready")
        x1_ready, x1_turned = sem("x1_ready"), sem("x1_turned")
        x1h_ready, x1l_ready = sem("x1h_ready"), sem("x1l_ready")
        x1b_ready = sem("x1b_ready")
        rows_done = sem("rows_done")
        rows_even, rows_odd = sem("rows_even"), sem("rows_odd")
        back = sem("back")
        relu_ready = sem("relu_ready")
        hxh_ready, hxl_ready = sem("hxh_ready"), sem("hxl_ready")
        bn_ready, xh_done = sem("bn_ready"), sem("xh_done")
        xn_turned, xn_even, xn_odd = sem("xn_turned"), sem("xn_even"), sem("xn_odd")
        cx_done, cxh_ready, cxl_ready = sem("cx_done"), sem("cxh_ready"), sem("cxl_ready")
        h2_step = sem("h2_step")
        out_done, y_ready = sem("out_done"), sem("y_ready")
        dve_step, pool_step = sem("dve_step"), sem("pool_step")

        def source(n, count):
            if n < WIN:
                return wp[P * n:P * (n + count), :]
            if n < CONV:
                return w_in[P * (n - WIN):P * (n - WIN + count), :]
            if n < WOUT:
                return wc[P * (n - CONV):P * (n - CONV + count), :]
            return w_out[P * (n - WOUT):P * (n - WOUT + count), :]

        def raw(n):
            first, _, cols, at, loaded, value = next(t for t in loads if t[0] <= n < t[0] + t[1])
            return ring[:, at + (n - first) * cols:at + (n - first + 1) * cols], loaded, value

        def low_told(n):
            pooled = by_pool_before(n + 1)
            return (low_ready_pool, pooled) if by_pool(n) else (low_ready, n + 1 - pooled)

        def part(tensor, n):
            return tensor[:, buffer(n)[0]]

        block = ctx.enter_context(nc.Block())

        @block.sync
        def _(sp):
            sp.dma_start(erow_i, edges).then_inc(erow_loaded, 16)
            sp.dma_start(ecol_i, ecols).then_inc(ecol_loaded, 16)
            owner = [0] * RING
            for n, count, cols, at, loaded, _ in loads:
                free = max(owner[at:at + count * cols])
                if free:
                    sp.wait_ge(low_ready, free - by_pool_before(free))
                    if by_pool_before(free):
                        sp.wait_ge(low_ready_pool, by_pool_before(free))
                sp.dma_start(ring[:, at:at + count * cols].rearrange("p (k n) -> p k n", n=cols),
                             source(n, count).rearrange("(k p) n -> p k n", p=P)).then_inc(loaded, 16)
                owner[at:at + count * cols] = [n + count] * (count * cols)
                if n == 8:
                    sp.dma_start(x_nat[0:N, :], x).then_inc(x_loaded, 16)
                    for k in range(4):
                        sp.dma_start(rows_sb[32 * k:32 * k + 1, :], rows[k:k + 1, :]).then_inc(rows_loaded, 16)
            for h in range(2):
                sp.wait_ge(y_ready, h + 1)
                sp.dma_start(out[:, 512 * h:512 * (h + 1)], y_out[:, 512 * h:512 * (h + 1)]).then_inc(stored[h], 16)
            for h in range(2):
                sp.wait_ge(stored[h], 16)

        @block.gpsimd
        def _(pool):
            steps = [0]

            def step(ins):
                steps[0] += 1
                ins.then_inc(pool_step, 1)
                pool.wait_ge(pool_step, steps[0])

            step(pool.memset(ident[:, :], 0.0))
            pool.affine_select(out=ident[:, :], in_=ident[:, :], compare_op=ALU.not_equal, fill=1.0, base=0,
                               pattern=[[-1, P]], channel_multiplier=1).then_inc(consts_ready, 1)
            pool.memset(ones[:, :], 1.0).then_inc(consts_ready, 1)
            pool.memset(ones_bf, 1.0).then_inc(consts_ready, 1)
            step(pool.memset(keyw, 1.0))
            pool.memset(keyw[0:1, :], float(N)).then_inc(keyw_ready, 1)
            step(pool.memset(tri, 1.0))
            pool.affine_select(out=tri, in_=tri, compare_op=ALU.is_gt, fill=0.0, base=0,
                               pattern=[[-1, P]], channel_multiplier=1).then_inc(consts_ready, 1)
            iota_i = work[:, 6368:6944].bitcast(i32)
            step(pool.iota(iota_i, [[1, R * N]], base=0, channel_multiplier=0))
            pool.tensor_copy(iota, iota_i).then_inc(consts_ready, 1)

            def split(n):
                pool.wait_ge(high_ready, n + 1)
                pool.tensor_tensor(part(w_low, n), raw(n)[0], part(w_high, n).bitcast(f32),
                                   ALU.subtract).then_inc(low_ready_pool, 1)

            def mix(l, r):
                to = ct[:, l * B * N:(l + 1) * B * N].rearrange("p (b n) -> p b n", n=N)
                term_v = term.rearrange("p (b n) -> p b n", n=N)
                comp = par[0:N, C_COMP + (l * R + r) * B:C_COMP + (l * R + r + 1) * B]
                last = pool.tensor_tensor(term_v if r else to,
                                          adj[:, N * r:N * (r + 1)].unsqueeze(1).to_broadcast([N, B, N]),
                                          comp.unsqueeze(2).to_broadcast([N, B, N]), ALU.mult)
                step(last)
                if r:
                    last = pool.tensor_tensor(to, to, term_v, ALU.add)
                    if r < R - 1:
                        step(last)
                    else:
                        last.then_inc(ct_ready, 1)

            for n in (3, 6, 8, 10, 12, 14, 16):
                split(n)
            pool.wait_ge(onehot_ready, 3 * ET)
            pool.wait_ge(dup_ready, 1)
            pool.tensor_tensor(Dw, Dh, dupcode.unsqueeze(2).to_broadcast([P, ET, N]), ALU.mult).then_inc(dw_ready, 1)
            for n in (20, 25, 28, 30):
                split(n)
            pool.wait_ge(codes_copied, 1)
            pool.wait_ge(w4_ready, 1)
            step(pool.tensor_scalar(mtmp, mcode, 0.0, 4.0, ALU.is_equal, ALU.mult))
            step(pool.tensor_tensor(mtmp, mtmp, ident[0:N, 0:N], ALU.mult))
            step(pool.tensor_tensor(mcode, mcode, mtmp, ALU.add))
            step(pool.tensor_scalar(mask, mcode, 0.0, NEG, ALU.is_equal, ALU.mult))
            for k in range(4):
                step(pool.tensor_scalar(mtmp, mcode, float(k + 1), w4[0:N, k:k + 1], ALU.is_equal, ALU.mult))
                last = pool.tensor_tensor(mask, mask, mtmp, ALU.add)
                if k < 3:
                    step(last)
            last.then_inc(mask_ready, 1)
            split(35)
            pool.wait_ge(adj_ready, R)
            pool.wait_ge(par_loaded, 16)
            mix(0, 0)
            mix(0, 1)

            def scale(k):
                pool.wait_ge(recips, k + 1)
                pool.tensor_tensor(pr[:, k], pr[:, k], rs[0:N, k].unsqueeze(2).to_broadcast([N, 4, N]),
                                   ALU.mult).then_inc(probs_ready, 1)

            split(40)
            split(42)
            for k in range(4):
                pool.wait_ge(maxed, k + 1)
                pool.tensor_tensor(pr[:, k], pr[:, k], mx[0:N, k].unsqueeze(2).to_broadcast([N, 4, N]),
                                   ALU.subtract).then_inc(shifted, 1)
                if k > 1:
                    scale(k - 2)
            scale(2)
            scale(3)
            split(WO + 1)
            split(WO + 2)
            mix(0, 2)
            split(WIN + 1)
            for r in range(3, R):
                mix(0, r)
            for n in range(WIN + 2, BLOCKS):
                if n == CONV:
                    pool.wait_ge(row_copied, 4)
                    pool.tensor_tensor(x1b, x1b, x_nat[0:N, :], ALU.add).then_inc(x1b_ready, 1)
                if by_pool(n):
                    split(n)
                    if n % 5 == 0 and CONV < n <= CONV + 5 * R:
                        mix(1, (n - CONV) // 5)

        @block.scalar
        def _(act):
            act.dma_start(turnT[:, :], xt).then_inc(xt_loaded, 16)
            act.dma_start(par[:, :], params).then_inc(par_loaded, 16)

            def split(n):
                view, loaded, value = raw(n)
                act.wait_ge(loaded, value)
                if buffer(n)[1]:
                    act.wait_ge(used, buffer(n)[1])
                act.activation(part(w_high, n), view, ACT.Copy).then_inc(high_ready, 1)

            def copy(dst, src, signal):
                act.activation(dst, src, ACT.Copy).then_inc(signal, 1)

            act.wait_ge(xt_loaded, 16)
            copy(x_high[:, :], turnT[:, :], xh_ready)

            def rows_of(m):
                act.wait_ge(used, FB * (m + 1))
                if m >= 1:
                    act.wait_ge(turned, 2 * m)
                for h in range(2):
                    copy(flat_sb[0:N, 512 * h:512 * (h + 1)], ps[0:N, ACC[m % 2][h], :], flat_ready)

            def high_of(m):
                for h in range(2):
                    act.wait_ge(turned_ready, 2 * m + h + 1)
                    copy(hh[:, SLOT[m], 4 * h:4 * h + 4, :], turned_v[:, 4 * h:4 * h + 4, :], hh_ready)

            for n in range(WO):
                split(n)
                if n == 5:
                    act.wait_ge(w4_abs, 1)
                    act.activation(w4e, w4n, ACT.Exp).then_inc(w4_exp, 1)
                    act.wait_ge(w4_exp, 1)
                    act.activation(w4l, w4e, ACT.Ln, bias=1.0).then_inc(w4_log, 1)
                if n == FB * V1 + 4:
                    act.activation(dummy, ident[:, 0:1], ACT.Exp)
                m, i = divmod(n, FB)
                if m >= 1 and i == (1 if m == V2 else 3):
                    rows_of(m - 1)
                if m - 1 in SLOT and i == (1 if m == V2 else 7):
                    high_of(m - 1)
                if m == V2 and 3 <= i < 7:
                    act.wait_ge(shifted, i - 2)
                    act.activation(pr[:, i - 3], pr[:, i - 3], ACT.Exp).then_inc(expd, 1)
            split(WO)

            def even_probs(h):
                act.wait_ge(probs_turned, h + 1)
                copy(prT[:, 2 * h], quad(PROBS_T[2 * h])[0:N], prT_even)

            def high_of_mixed(h):
                act.wait_ge(mixed_ready, h + 1)
                copy(hh[:, 0, 4 * h:4 * h + 4, :], turned_v[:, 4 * h:4 * h + 4, :], oh_ready)

            act.wait_ge(v2_done, 1)
            copy(v2[:, 0:512], ps[0:N, ACC[1][0], :], v2_even)
            even_probs(0)
            even_probs(1)
            split(WO + 1)
            high_of_mixed(0)
            split(WO + 2)
            high_of_mixed(1)
            for n in range(WO + 3, WIN + AHEAD):
                split(n)
                if n == WO + 5:
                    act.activation(dummy, ident[:, 0:1], ACT.Sqrt)

            def sqrt(v, parts, o, count):
                act.wait_ge(var_ready, v)
                act.activation(std[0:parts, o:o + count], mv[0:parts, o:o + count, 1], ACT.Sqrt,
                               bias=eps[0:parts, :]).then_inc(std_ready, 1)

            sqrt(1, N, 0, 1)
            for h in range(2):
                act.wait_ge(x1_turned, h + 1)
                copy(xh[:, 4 * h:4 * h + 4, :], quad(EDGE[h]), x1h_ready)
            for n in range(WIN + AHEAD, CONV + 1):
                split(n)
                if n < WIN + AHEAD + 4:
                    k, h = divmod(n - (WIN + AHEAD), 2)
                    act.wait_ge(row_spread, 2 * k + h + 1)
                    copy((gamma_b, x1b)[k][:, 512 * h:512 * (h + 1)], ps[0:N, (TURN, ACC[1])[k][h], :], row_copied)

            def from_rows(c):
                act.wait_ge(rows_done, c + 1)
                copy(flat_sb[0:N, 0:384], ps[0:N, ACC[0][0], 0:384], rows_even)
                to, bias = (rT, C_CONV + (c - 1) * DB) if c else (hx, C_BIN)
                for h in range(2):
                    act.wait_ge(back, 2 * c + h + 1)
                    for o in range(3 * h, 3 * h + 3):
                        act.activation(to[:, o, :], quad(TURN[h])[:, o % 3], ACT.Relu,
                                       bias=par[:, bias + o:bias + o + 1]).then_inc(relu_ready, 1)
                    if c == 0:
                        act.wait_ge(relu_ready, 3 * (h + 1))
                        copy(xh[:, 3 * h:3 * h + 3, :], hx[:, 3 * h:3 * h + 3, :], hxh_ready)
                    if h == 0:
                        split(CONV + c * LAYER + 1)

            from_rows(0)
            for l in range(L):
                base = CONV + l * LAYER
                for k in range(4 if l else 2, LAYER + 1):
                    split(base + k)
                    if k == 4:
                        act.wait_ge(xn_turned, 2 * l + 1)
                        copy(xn[:, 0:512], ps[0:N, EDGE[0], :], xn_even)
                    if k == DB + 2:
                        for i in range(DB):
                            act.wait_ge(cx_done, DB * l + i + 1)
                            copy(cxh[:, i], quad(CX[i % 4]), cxh_ready)
                from_rows(l + 1)
                for h in range(2):
                    sqrt(2 * l + h + 2, P, 3 * h, 3)
                    if h == 0:
                        split(base + LAYER + 2)
                    act.wait_ge(bn_ready, 2 * l + h + 1)
                    for o in range(3 * h, 3 * h + 3):
                        act.activation(xh[:, o, :], rT[:, o, :], ACT.Identity, scale=bn_a[:, o:o + 1],
                                       bias=bn_c[:, o:o + 1]).then_inc(xh_done, 1)
                    if h == 0:
                        split(base + LAYER + 3)
            for n in range(WOUT + 4, BLOCKS):
                split(n)
            sqrt(2 * L + 2, N, 0, 1)
            sqrt(2 * L + 3, N, 0, 1)

        @block.vector
        def _(dve):
            steps = [0]

            def step(ins):
                steps[0] += 1
                ins.then_inc(dve_step, 1)
                dve.wait_ge(dve_step, steps[0])

            def split(n):
                if by_pool(n):
                    return
                dve.wait_ge(high_ready, n + 1)
                dve.tensor_tensor(part(w_low, n), raw(n)[0], part(w_high, n).bitcast(f32),
                                  ALU.subtract).then_inc(low_ready, 1)

            step(dve.memset(eps, EPS))
            dve.wait_ge(erow_loaded, 16)
            dve.tensor_copy(erow, erow_i).then_inc(erow_ready, 1)
            dve.wait_ge(xh_ready, 1)
            dve.tensor_tensor(x_low[:, :], turnT[:, :], x_high[:, :].bitcast(f32), ALU.subtract).then_inc(xl_ready, 1)
            dve.wait_ge(ecol_loaded, 16)
            step(dve.tensor_copy(ecol, ecol_i))
            dve.scalar_tensor_tensor(relcol, typ6, float(N), dst, ALU.mult, ALU.add)
            step(dve.scalar_tensor_tensor(keycol, src, float(N), dst, ALU.mult, ALU.add))

            def mask_scores(k):
                dve.wait_ge(scored, k + 1)
                step(dve.scalar_tensor_tensor(pr[:, k], quad(4 + k)[0:N], SCALE,
                                              mask.unsqueeze(1).to_broadcast([N, 4, N]), ALU.mult, ALU.add))
                dve.tensor_reduce(mx[0:N, k], pr[:, k], AX.X, ALU.max).then_inc(maxed, 1)

            def total(k):
                dve.wait_ge(expd, k + 1)
                step(dve.tensor_reduce(sm[0:N, k], pr[:, k], AX.X, ALU.add))
                dve.reciprocal(rs[0:N, k], sm[0:N, k]).then_inc(recips, 1)

            def bias_of(m, banks):
                to = {Q2: q2T, K2: k2T}.get(m, turned_v)
                for h in range(2):
                    dve.wait_ge(turned, 2 * m + h + 1)
                    bias = par[:, FB * m + 4 * h:FB * m + 4 * h + 4]
                    dve.tensor_tensor(to[:, 4 * h:4 * h + 4, :], quad(banks[h]),
                                      bias.unsqueeze(2).to_broadcast([P, 4, N]), ALU.add).then_inc(turned_ready, 1)

            def low_of(m):
                for h in range(2):
                    dve.wait_ge(hh_ready, 2 * SLOT[m] + h + 1)
                    dve.tensor_tensor(hl[:, SLOT[m], 4 * h:4 * h + 4, :], turned_v[:, 4 * h:4 * h + 4, :],
                                      hh[:, SLOT[m], 4 * h:4 * h + 4, :].bitcast(f32),
                                      ALU.subtract).then_inc(hl_ready, 1)

            etw = par[:, C_ETW:C_ETW + 4]
            for n in range(WO):
                split(n)
                if n == 0:
                    dve.wait_ge(par_loaded, 16)
                    step(dve.tensor_scalar(w4n, etw, -1.0, None, ALU.mult))
                    dve.tensor_tensor(w4n, w4n, etw, ALU.min).then_inc(w4_abs, 1)
                    dve.wait_ge(keys_spread, 1)
                    dve.wait_ge(consts_ready, 5)
                if n == 3:
                    step(dve.tensor_scalar(code4, typ5, 0.0, 4.0, ALU.is_equal, ALU.mult))
                    step(dve.tensor_tensor(code, code4, typ5, ALU.add))
                    for t in range(1, ET):
                        dve.tensor_scalar(code[:, t:t + 1], code[:, t:t + 1], float(16 ** t), None, ALU.mult)
                if 1 <= n <= ET // 2:
                    for t in (2 * n - 2, 2 * n - 1):
                        dve.scalar_tensor_tensor(later[:, t, :], ps[:, 4 + t // 4, P * (t % 4):P * (t % 4 + 1)],
                                                 keycol[:, t:t + 1], tri, ALU.is_equal,
                                                 ALU.mult).then_inc(later_ready, 1)
                if n == 7:
                    dve.wait_ge(w4_log, 1)
                    dve.scalar_tensor_tensor(w4, etw, 0.0, w4l, ALU.max, ALU.add).then_inc(w4_ready, 1)
                if 5 <= n < 5 + ET:
                    for hot, count, col in ((S, N, src), (Dh, N, dst), (D6, R * N, relcol)):
                        dve.tensor_scalar(hot[:, n - 5, :], iota[:, 0:count], col[:, n - 5:n - 4], None,
                                          ALU.is_equal).then_inc(onehot_ready, 1)
                if n == DUPS_AT + BEHIND:
                    dve.wait_ge(dups_done, 1)
                    dve.scalar_tensor_tensor(dupcode, ps[:, EDGE[1], 0:ET], 0.0, code, ALU.is_equal,
                                             ALU.mult).then_inc(dup_ready, 1)
                if n == ADJ_AT + BEHIND:
                    for h in range(2):
                        dve.wait_ge(adj_done, h + 1)
                        dve.tensor_copy(adj[:, 288 * h:288 * (h + 1)], ps[0:N, EDGE[h], 0:288]).then_inc(adj_copied, 1)
                if n == CNT_AT + BEHIND:
                    for h in range(2):
                        dve.wait_ge(cnt_done, h + 1)
                        last = dve.tensor_scalar(cnt[:, 288 * h:288 * (h + 1)], ps[0:N, EDGE[h], 0:288], 1.0, None,
                                                 ALU.max)
                        last.then_inc(cnt_copied, 1)
                r = n - (CNT_AT + BEHIND + 1)
                if 0 <= r < R:
                    dve.wait_ge(cnt_copied, 2)
                    relation = slice(N * r, N * (r + 1))
                    step(dve.reciprocal(cnt[:, relation], cnt[:, relation]))
                    dve.tensor_tensor(adj[:, relation], adj[:, relation], cnt[:, relation],
                                      ALU.mult).then_inc(adj_ready, 1)
                if n == CODES_AT + BEHIND:
                    dve.wait_ge(codes_done, 1)
                    step(dve.tensor_copy(msum, ps[0:N, EDGE[0], 0:N]))
                    step(dve.tensor_scalar(mbits.bitcast(i32), msum.bitcast(i32), 22, 7,
                                           ALU.logical_shift_right, ALU.bitwise_and))
                    step(dve.tensor_copy(mlead, mbits.bitcast(i32)))
                    step(dve.tensor_scalar(mtmp, mlead, 6.0, -7.0, ALU.is_equal, ALU.mult))
                    step(dve.scalar_tensor_tensor(mtmp, mlead, 2.0, mtmp, ALU.add, ALU.add))
                    dve.scalar_tensor_tensor(mcode, msum, 0.0, mtmp, ALU.is_gt, ALU.mult).then_inc(codes_copied, 1)
                m, i = divmod(n, FB)
                if 1 <= m < V2 and i == (5 if m == V1 else 6):
                    bias_of(m - 1, TURN)
                if m in (Q1 + 1, K1 + 1) and i == 7:
                    low_of(m - 1)
                if m == V2:
                    if i == 0:
                        dve.wait_ge(mask_ready, 1)
                    if i == 1:
                        bias_of(V1, ACC[0])
                        low_of(V1)
                    if i < 4:
                        mask_scores(i)
                    if 3 <= i < 7:
                        total(i - 3)
            split(WO)

            def odd_probs(h):
                dve.wait_ge(probs_turned, h + 1)
                dve.tensor_copy(prT[:, 2 * h + 1], quad(PROBS_T[2 * h + 1])[0:N]).then_inc(prT_odd, 1)

            def bias_of_mixed(h):
                bias = par[:, FB * V2 + 4 * h:FB * V2 + 4 * h + 4]
                dve.wait_ge(mixed, h + 1)
                dve.tensor_tensor(turned_v[:, 4 * h:4 * h + 4, :], quad(ACC[1][h]),
                                  bias.unsqueeze(2).to_broadcast([P, 4, N]), ALU.add).then_inc(mixed_ready, 1)

            def low_of_mixed(h):
                dve.wait_ge(oh_ready, h + 1)
                dve.tensor_tensor(hl[:, 0, 4 * h:4 * h + 4, :], turned_v[:, 4 * h:4 * h + 4, :],
                                  hh[:, 0, 4 * h:4 * h + 4, :].bitcast(f32), ALU.subtract).then_inc(ol_ready, 1)

            odd_probs(0)
            odd_probs(1)
            dve.wait_ge(used, WO)
            dve.tensor_copy(v2[:, 512:1024], ps[0:N, ACC[1][1], :]).then_inc(v2_odd, 1)
            bias_of_mixed(0)
            low_of_mixed(0)
            bias_of_mixed(1)
            low_of_mixed(1)
            for n in range(WO + AHEAD, WIN + AHEAD):
                split(n)

            def half_stats(h, view):
                step(dve.bn_stats(st[0:N, h, :], view))

            def half_std():
                dve.bn_aggr(mv[0:N, 0, :], st[0:N, 0:2, :]).then_inc(var_ready, 1)

            def half_rstd(v):
                dve.wait_ge(std_ready, v)
                step(dve.reciprocal(rstd[0:N, 0:1], std[0:N, 0:1]))

            def normalize(to, view, signal):
                dve.tensor_scalar(to, view, mv[0:N, 0, 0:1], rstd[0:N, 0:1],
                                  ALU.subtract, ALU.mult).then_inc(signal, 1)

            dve.wait_ge(x_loaded, 16)
            for h in range(2):
                half = slice(512 * h, 512 * (h + 1))
                dve.wait_ge(*((attended, 1), (used, WIN))[h])
                step(dve.tensor_tensor(r1[:, half], ps[0:N, ACC[0][h], :], x_nat[0:N, half], ALU.add))
                half_stats(h, r1[:, half])
            half_std()
            half_rstd(1)
            for h in range(2):
                half = slice(512 * h, 512 * (h + 1))
                normalize(x_nat[0:N, half], r1[:, half], x1_ready)
            for h in range(2):
                dve.wait_ge(x1h_ready, h + 1)
                dve.tensor_tensor(xl[:, 4 * h:4 * h + 4, :], quad(EDGE[h]), xh[:, 4 * h:4 * h + 4, :].bitcast(f32),
                                  ALU.subtract).then_inc(x1l_ready, 1)
            for n in range(WIN + AHEAD, CONV + AHEAD):
                split(n)

            def rest_of_rows(c):
                dve.wait_ge(used, CONV + c * LAYER)
                dve.tensor_copy(flat_sb[0:N, 384:768], ps[0:N, ACC[0][1], 0:384]).then_inc(rows_odd, 1)

            def low_of_hx(told, value, h):
                dve.wait_ge(told, value)
                dve.tensor_tensor(xl[:, 3 * h:3 * h + 3, :], hx[:, 3 * h:3 * h + 3, :],
                                  xh[:, 3 * h:3 * h + 3, :].bitcast(f32), ALU.subtract).then_inc(hxl_ready, 1)

            rest_of_rows(0)
            for h in range(2):
                low_of_hx(hxh_ready, h + 1, h)
            for l in range(L):
                base = CONV + l * LAYER
                for k in range(AHEAD, LAYER + AHEAD):
                    split(base + k)
                    if k == 4:
                        dve.wait_ge(xn_turned, 2 * l + 2)
                        dve.tensor_copy(xn[:, 512:768], ps[0:N, EDGE[1], 0:256]).then_inc(xn_odd, 1)
                    if k == DB + 2:
                        for i in range(DB):
                            dve.wait_ge(cxh_ready, DB * l + i + 1)
                            dve.tensor_tensor(cxl[:, i], quad(CX[i % 4]), cxh[:, i].bitcast(f32),
                                              ALU.subtract).then_inc(cxl_ready, 1)
                rest_of_rows(l + 1)
                for h in range(2):
                    third = slice(3 * h, 3 * h + 3)
                    gamma, beta = (par[:, at + l * DB + 3 * h:at + l * DB + 3 * h + 3] for at in (C_GAMMA, C_BETA))
                    dve.wait_ge(relu_ready, (l + 1) * DB + 3 * (h + 1))
                    step(dve.tensor_tensor(rT[:, third, :], rT[:, third, :], hx[:, third, :], ALU.add))
                    for o in range(3 * h, 3 * h + 3):
                        last = dve.bn_stats(st[:, o, :], rT[:, o, :])
                    step(last)
                    for o in range(3 * h, 3 * h + 3):
                        last = dve.bn_aggr(mv[:, o, :], st[:, o, :])
                    last.then_inc(var_ready, 1)
                    dve.wait_ge(var_ready, 2 * l + h + 2)
                    step(dve.tensor_tensor(bn_m[:, third], mv[:, third, 0], gamma, ALU.mult))
                    dve.wait_ge(std_ready, 2 * l + h + 2)
                    step(dve.reciprocal(rstd[:, third], std[:, third]))
                    dve.tensor_tensor(bn_a[:, third], rstd[:, third], gamma, ALU.mult)
                    step(dve.tensor_tensor(bn_m[:, third], bn_m[:, third], rstd[:, third], ALU.mult))
                    dve.tensor_tensor(bn_c[:, third], beta, bn_m[:, third], ALU.subtract).then_inc(bn_ready, 1)
                    dve.wait_ge(bn_ready, 2 * l + h + 1)
                    for o in range(3 * h, 3 * h + 3):
                        last = dve.tensor_scalar(hx[:, o, :], rT[:, o, :], bn_a[:, o:o + 1], bn_c[:, o:o + 1],
                                                 ALU.mult, ALU.add)
                    step(last)
                    low_of_hx(xh_done, DB * l + 3 * (h + 1), h)
            for n in range(WOUT + AHEAD, BLOCKS):
                split(n)
            for h in range(2):
                dve.wait_ge(*((out_done, 1), (used, BLOCKS))[h])
                half_stats(h, ps[0:N, ACC[0][h], :])
            half_std()
            dve.wait_ge(x1b_ready, 1)
            dve.wait_ge(var_ready, 2 * L + 2)
            halves = [slice(512 * h, 512 * (h + 1)) for h in range(2)]
            for h in range(2):
                dve.scalar_tensor_tensor(h2[:, halves[h]], ps[0:N, ACC[0][h], :], mv[0:N, 0, 0:1],
                                         gamma_b[:, halves[h]], ALU.subtract, ALU.mult).then_inc(h2_step, 1)
            half_rstd(2 * L + 2)
            for h in range(2):
                dve.wait_ge(h2_step, h + 1)
                dve.scalar_tensor_tensor(h2[:, halves[h]], h2[:, halves[h]], rstd[0:N, 0:1], x1b[:, halves[h]],
                                         ALU.mult, ALU.add).then_inc(h2_step, 1)
            for h in range(2):
                dve.wait_ge(h2_step, h + 3)
                last = dve.bn_stats(st[0:N, h, :], h2[:, halves[h]])
            step(last)
            half_std()
            half_rstd(2 * L + 3)
            for h in range(2):
                normalize(y_out[:, halves[h]], h2[:, halves[h]], y_ready)

        @block.tensor
        def _(pe):
            def keep_warm(count, bank):
                for _ in range(count):
                    pe.matmul(ps[:, bank, 0:2 * P], ident_bf[:, 0:P], ident_bf, start=True, stop=True,
                              skip_group_check=True)

            ident_bf = ident[:, :].bitcast(bf16)
            pe.wait_ge(consts_ready, 1)
            keep_warm(WARMERS["start"], 0)
            pe.wait_ge(consts_ready, 5)
            pe.wait_ge(erow_ready, 1)
            pe.wait_ge(keyw_ready, 1)
            for c in range(3):
                last = pe.matmul(ps[:, 4 + c, :], keyw, erow[:, 512 * c:512 * (c + 1)], start=True, stop=True)
            last.then_inc(keys_spread, 1)

            def product(n, buf, high, low, first, end, layer=0, done=None, halves=(0, 1)):
                cols = F if n < WIN or n >= WOUT else D
                w = cols // 2
                pe.wait_ge(high_ready, layer * LAYER + (n + 1))
                for weight, left in ((w_high, high), (w_high, low), (w_low, high)):
                    if weight is w_low:
                        told, value = low_told(n)
                        per_layer = by_pool_before(CONV + LAYER) - by_pool_before(CONV)
                        if told is low_ready:
                            per_layer = LAYER - per_layer
                        pe.wait_ge(told, layer * per_layer + value)
                    for h in halves:
                        last = pe.matmul(ps[0:N, buf[h], 0:w], left, part(weight, n)[:, w * h:w * (h + 1)],
                                         start=first and weight is w_high and left is high,
                                         stop=end and weight is w_low,
                                         skip_group_check=True)
                        if done is not None and weight is w_low and h == 0:
                            last.then_inc(done, 1)
                if 1 in halves:
                    last.then_inc(used, 1)

            def close(end, tail, buf, left, done, layer=0, back=None):
                for h in range(2):
                    for n in range(end - tail, end):
                        last = n == end - 1
                        if h == 1 and last and back is not None:
                            back()
                        high, low = left(n)
                        product(n, buf, high, low, False, last, layer=layer, done=done if h == 0 and last else None,
                                halves=(h,))

            def turn(m, banks):
                if 1 <= m < V1:
                    pe.wait_ge(turned_ready, 2 * m)
                for i in range(FB):
                    if i % 4 == 0:
                        pe.wait_ge(flat_ready, 2 * m + i // 4 + 1)
                    last = pe.transpose(quad(banks[i // 4])[:, i % 4], flat_sb[0:N, P * i:P * (i + 1)],
                                        ident[0:N, 0:N])
                    if i % 4 == 3:
                        last.then_inc(turned, 1)

            for n in range(WO - 2):
                m, i = divmod(n, FB)
                if n == 0:
                    pe.wait_ge(xl_ready, 1)
                if n in (FB * V2 - 2, FB * V2 - 1):
                    half = n - (FB * V2 - 2)
                    pe.wait_ge(turned_ready, 2 * (K2 + 1))
                    pe.wait_ge(codes_copied, 1)
                    for c in range(4):
                        for odd in range(2):
                            hd = slice(HD * odd, HD * (odd + 1))
                            last = pe.matmul(quad(4 + 2 * half + odd)[0:N, c], q2T[hd, 4 * half + c, :],
                                             k2T[hd, 4 * half + c, :], start=True, stop=True)
                            if c == 3:
                                last.then_inc(scored, 1)
                if n == FB * V2:
                    turn(V1, ACC[0])
                    keep_warm(WARMERS["v2"], ACC[1][0])
                if i % 4 == 0 and m in (Q2, K2, V2):
                    pe.wait_ge(hl_ready, {Q2: 0, K2: 2, V2: 4}[m] + i // 4 + 1)
                slot = SLOT.get({Q2: Q1, K2: K1, V2: V1}.get(m))
                high, low = (xh, xl) if slot is None else (hh[:, slot], hl[:, slot])
                product(n, ACC[m % 2], high[:, i, :], low[:, i, :], i == 0, i == FB - 1)
                if 1 <= m < V2 and i == 2:
                    if m == 1:
                        pe.wait_ge(later_ready, ET)
                    turn(m - 1, TURN)
                if n == DUPS_AT:
                    pe.wait_ge(later_ready, ET)
                    for t in range(ET):
                        last = pe.matmul(ps[:, EDGE[1], t:t + 1], later[:, t, :], ones_bf, start=True, stop=True)
                    last.then_inc(dups_done, 1)
                if n == ADJ_AT:
                    pe.wait_ge(onehot_ready, 3 * ET)
                    pe.wait_ge(dup_ready, 1)
                    for h in range(2):
                        for t in range(ET):
                            last = pe.matmul(ps[0:N, EDGE[h], 0:288], S[:, t, :], D6[:, t, 288 * h:288 * (h + 1)],
                                             start=(t == 0), stop=(t == ET - 1))
                        last.then_inc(adj_done, 1)
                if n == CNT_AT:
                    pe.wait_ge(adj_copied, 2)
                    for h in range(2):
                        pe.matmul(ps[0:N, EDGE[h], 0:288], ones[0:N, :], adj[:, 288 * h:288 * (h + 1)],
                                  start=True, stop=True).then_inc(cnt_done, 1)
                if n == CODES_AT:
                    pe.wait_ge(cnt_copied, 2)
                    pe.wait_ge(dw_ready, 1)
                    for t in range(ET):
                        last = pe.matmul(ps[0:N, EDGE[0], 0:N], S[:, t, :], Dw[:, t, :],
                                         start=(t == 0), stop=(t == ET - 1))
                    last.then_inc(codes_done, 1)

            def turn_probs(h):
                pe.wait_ge(probs_ready, 2 * h + 2)
                for k in (2 * h, 2 * h + 1):
                    for c in range(4):
                        last = pe.transpose(quad(PROBS_T[k])[0:N, c], pr[:, k, c], ident[0:N, 0:N])
                last.then_inc(probs_turned, 1)

            def mix_values(h):
                pe.wait_ge((v2_even, v2_odd)[h], 1)
                pe.wait_ge(prT_even, h + 1)
                pe.wait_ge(prT_odd, h + 1)
                for c in range(4):
                    for odd in range(2):
                        head = 8 * h + 2 * c + odd
                        last = pe.matmul(quad(ACC[1][h])[HD * odd:HD * (odd + 1), c], v2[:, HD * head:HD * (head + 1)],
                                         prT[:, 2 * h + odd, c], start=True, stop=True)
                last.then_inc(mixed, 1)

            def spread(row, h, bank, stop):
                return pe.matmul(ps[0:N, bank, :], ones[32 * row:32 * row + 1, :],
                                 rows_sb[32 * row:32 * row + 1, 512 * h:512 * (h + 1)],
                                 start=True, stop=stop, skip_group_check=True)

            pe.wait_ge(rows_loaded, 64)
            for h in range(2):
                spread(0, h, ACC[0][h], False)
            close(WO, 2, ACC[1], lambda n: (hh[:, SLOT[V1], n % FB, :], hl[:, SLOT[V1], n % FB, :]), v2_done,
                  back=lambda: [turn_probs(h) for h in range(2)])
            mix_values(0)
            mix_values(1)
            keep_warm(WARMERS["wo"], TURN[0])
            for i in range(FB - 2):
                if i % 4 == 0:
                    pe.wait_ge(ol_ready, i // 4 + 1)
                product(WO + i, ACC[0], hh[:, 0, i, :], hl[:, 0, i, :], False, False)
            close(WIN, 2, ACC[0], lambda n: (hh[:, 0, n - WO, :], hl[:, 0, n - WO, :]), attended)
            for k in range(2):
                for h in range(2):
                    spread(2 + k, h, (TURN, ACC[1])[k][h], True).then_inc(row_spread, 1)
            for i in range(FB):
                if i % 4 == 0:
                    pe.wait_ge(x1_ready, i // 4 + 1)
                last = pe.transpose(quad(EDGE[i // 4])[:, i % 4], x_nat[0:N, P * i:P * (i + 1)], ident[0:N, 0:N])
                if i % 4 == 3:
                    last.then_inc(x1_turned, 1)

            def back_from_rows(c, h):
                pe.wait_ge((rows_even, rows_odd)[h], c + 1)
                for o in range(3):
                    last = pe.transpose(quad(TURN[h])[:, o], flat_sb[0:N, P * (3 * h + o):P * (3 * h + o + 1)],
                                        ident[0:N, 0:N])
                last.then_inc(back, 1)

            keep_warm(WARMERS["w_in"], ACC[0][0])
            pe.wait_ge(x1l_ready, 1)
            for i in range(FB - 4):
                product(WIN + i, ACC[0], xh[:, i, :], xl[:, i, :], i == 0, False)
            pe.wait_ge(x1l_ready, 2)
            pe.wait_ge(row_copied, 4)
            close(CONV, 4, ACC[0], lambda n: (xh[:, n - WIN, :], xl[:, n - WIN, :]), rows_done,
                  back=lambda: back_from_rows(0, 0))
            back_from_rows(0, 1)
            with pe.Fori(0, L) as l:
                keep_warm(WARMERS["layer"], CX[0])
                for h in range(2):
                    pe.wait_ge(hxl_ready, 2 * l + (h + 1))
                    for o in range(3 * h, 3 * h + 3):
                        last = pe.transpose(ps[0:N, EDGE[o // 4], P * (o % 4):P * (o % 4 + 1)], hx[:, o, :],
                                            ident[:, :])
                        if o in (3, DB - 1):
                            last.then_inc(xn_turned, 1)
                    for i in range(3 * h, 3 * h + 3):
                        product(CONV + i, ACC[0], xh[:, i, :], xl[:, i, :], i == 0, False, layer=l)
                pe.wait_ge(xn_even, l + 1)
                pe.wait_ge(xn_odd, l + 1)
                pe.wait_ge(ct_ready, l + 1)
                for i in range(DB):
                    if i >= 4:
                        pe.wait_ge(cxl_ready, l * DB + (i - 3))
                    pe.matmul(ps[:, CX[i % 4], 0:B * N], xn[:, P * i:P * (i + 1)],
                              ct[:, ds(l * (B * N), B * N)], start=True, stop=True).then_inc(cx_done, 1)
                for k in range(B * DB - 4):
                    b, i = divmod(k, DB)
                    if b == 0:
                        pe.wait_ge(cxl_ready, l * DB + (i + 1))
                    product(CONV + DB + k, ACC[0], cxh[:, i, b, :], cxl[:, i, b, :], False, False, layer=l)
                close(CONV + LAYER, 4, ACC[0],
                      lambda n: (cxh[:, (n - CONV) % DB, B - 1, :], cxl[:, (n - CONV) % DB, B - 1, :]), rows_done,
                      layer=l, back=lambda: back_from_rows(l + 1, 0))
                back_from_rows(l + 1, 1)
                keep_warm(WARMERS["layer end"], CX[0])
            for h in range(2):
                spread(1, h, ACC[0][h], False)
            keep_warm(WARMERS["w_out"], CX[0])
            for i in range(DB - 2):
                if i % 3 == 0:
                    pe.wait_ge(hxl_ready, 2 * L + i // 3 + 1)
                product(WOUT + i, ACC[0], xh[:, i, :], xl[:, i, :], False, False)
            pe.wait_ge(hxl_ready, 2 * (L + 1))
            close(BLOCKS, 2, ACC[0], lambda n: (xh[:, n - WOUT, :], xl[:, n - WOUT, :]), out_done)


def kernel(**a):
    import concourse.bacc as bacc
    from concourse.bass_utils import run_bass_kernel_spmd

    def cols(*vectors):
        return np.concatenate([v.reshape(-1, P).T for v in vectors], axis=1)

    def spread(v):
        return np.broadcast_to(v.reshape(1, -1), (P, v.size))

    a = {name: np.asarray(v) for name, v in a.items()}
    g0, g1 = "L0_gnn_", "L1_gnn_"
    edges = np.stack([a[n] for n in ("src", "dst", "edge_type_5", "edge_type_6")])
    arrays = {
        "x": a["x"],
        "xt": np.ascontiguousarray(a["x"].T.reshape(FB, P, N).transpose(1, 0, 2).reshape(P, FB * N)),
        "edges": edges[0:2],
        "ecols": np.ascontiguousarray(edges.reshape(4 * ET, P).T),
        "params": np.ascontiguousarray(np.concatenate(
            [cols(*[a[g0 + "b" + n] for n in ORDER], a[g1 + "b_in"], a[g1 + "conv_bias"],
                  a[g1 + "bn_gamma"], a[g1 + "bn_beta"]),
             spread(a[g1 + "comp"]), spread(a[g0 + "edge_type_weights"])], axis=1)),
        "rows": np.stack([a[g0 + "bo"], a[g1 + "b_out"], a[g1 + "ln_gamma"], a[g1 + "ln_beta"]]),
        "wp": np.concatenate([a[g0 + "w" + n].T for n in (*ORDER, "o")]),
        "w_in": a[g1 + "w_in"],
        "wc": np.concatenate([a[g1 + "root"][:, None], a[g1 + "basis"]], axis=1).reshape(L * LAYER * P, D),
        "w_out": a[g1 + "w_out"],
    }
    nc = bacc.Bacc("TRN2", target_bir_lowering=False, num_devices=1)
    aps = {n: nc.dram_tensor(f"in_{n}", v.shape, mybir.dt.from_np(v.dtype), kind="ExternalInput").ap()
           for n, v in arrays.items()}
    out = nc.dram_tensor("out", (N, F), mybir.dt.float32, kind="ExternalOutput").ap()
    gnn_kernel(nc, out=out, **aps)
    result = run_bass_kernel_spmd(nc, [{f"in_{n}": v for n, v in arrays.items()}], core_ids=[0])
    return result.results[0]["out"]
```
